# Optimizing a Trainium2 kernel written in Bass

```python
import numpy as np
import jax
import jax.numpy as jnp

def _softmax(x, axis=-1):
    return jax.nn.softmax(x, axis=axis)

def _gelu(x):
    return jax.nn.gelu(x, approximate=True)

def _silu(x):
    return jax.nn.silu(x)

def _sigmoid(x):
    return jax.nn.sigmoid(x)

def _layernorm(x, axis=-1, eps=1e-05):
    m = jnp.mean(x, axis=axis, keepdims=True)
    v = jnp.var(x, axis=axis, keepdims=True)
    return (x - m) / jnp.sqrt(v + eps)

def _scatter_add(tgt, idx, src, axis=0):
    return tgt.at[idx].add(src)

def _segment_sum(src, seg, n):
    return jax.ops.segment_sum(src, seg, n)
kernel_name = 'mk_xattn_ffn_d1_seqx_r4_a9b2b3'

def setup_inputs(seed: int=0):
    np.random.seed(seed)
    _w = jnp.asarray

    def _rec_inputs():
        import jax
        import jax.numpy as jnp
        _rk = jax.random.key(seed)
        x = -0.000125 + 0.9999 * jax.random.normal(jax.random.fold_in(_rk, 1), (4, 512, 512), jnp.float32)
        _lenS = 512 - jax.random.randint(jax.random.fold_in(_rk, 7), (4,), 0, max(1, 512 // 4) + 1, jnp.int32)
        _lenS2 = 512 - jax.random.randint(jax.random.fold_in(_rk, 8), (4,), 0, max(1, 512 // 4) + 1, jnp.int32)
        itok_BxS_13_99985 = jax.random.randint(jax.random.fold_in(_rk, 11), (4, 512), 13, 99986, jnp.int32)
        _ctx_2048P = jax.random.normal(jax.random.fold_in(_rk, 12), (4, 16, 512), jnp.float32)
        _ctx_2048c = jax.random.dirichlet(jax.random.fold_in(_rk, 512), 0.3 * jnp.ones((16,), jnp.float32), (4, 512))
        _ctx_2048t = jnp.einsum('bsk,bkd->bsd', _ctx_2048c, _ctx_2048P)
        _ctx_2048t = _ctx_2048t * jax.lax.rsqrt(jnp.mean(jnp.square(_ctx_2048t)) + 1e-12) * 0.953939
        ctx_2048 = 6.82029e-06 + 0.0200006 * (_ctx_2048t + 0.3 * jax.random.normal(jax.random.fold_in(_rk, 612), (4, 512, 512), jnp.float32))
        return (x, itok_BxS_13_99985, ctx_2048)
    x, itok_BxS_13_99985, ctx_2048 = _rec_inputs()

    def _L0_xattn_setup():
        import jax, jax.numpy as jnp
        import numpy as np
        B, S, D = (4, 1024, 512)
        E = 4
        F = 2048 // E
        VOCAB = 25000
        key = jax.random.key(seed)
        k1, k2, k3, k4, k5 = jax.random.split(key, 5)
        hidden_states = jax.random.normal(k1, (B, S, D), dtype=jnp.float32)
        token_ids = jax.random.randint(k2, (B, S), 0, VOCAB, dtype=jnp.int64)
        Wg = jax.random.normal(k3, (E, F, D), dtype=jnp.float32) * 0.02
        Wu = jax.random.normal(k4, (E, F, D), dtype=jnp.float32) * 0.02
        Wd = jax.random.normal(k5, (E, D, F), dtype=jnp.float32) * 0.02
        return {'hidden_states': hidden_states, 'token_ids': token_ids, 'Wg': Wg, 'Wu': Wu, 'Wd': Wd}
    _L0_xattn_all = _L0_xattn_setup()
    _L0_xattn_in = {k: v for k, v in _L0_xattn_all.items() if k in ()}
    del _L0_xattn_all

    def _L0_ffn_setup():
        import jax, jax.numpy as jnp
        import numpy as np
        B, S, H = (4, 512, 512)
        E = 8
        F = H // E
        TOPK = 2
        LORA_R = 16
        LORA_SCALE = 1.0
        key = jax.random.key(seed)
        ks = jax.random.split(key, 7)
        x = jax.random.normal(ks[0], (B, S, H), dtype=jnp.float32)
        G = jax.random.normal(ks[1], (H, E), dtype=jnp.float32)
        gate_w = jax.random.normal(ks[2], (E, F, H), dtype=jnp.float32) * np.float32(np.sqrt(2.0 / H))
        up_w = jax.random.normal(ks[3], (E, F, H), dtype=jnp.float32) * np.float32(np.sqrt(2.0 / H))
        down_w = jax.random.normal(ks[4], (E, H, F), dtype=jnp.float32) * np.float32(np.sqrt(2.0 / F))
        lora_A = jax.random.normal(ks[5], (E, LORA_R, H), dtype=jnp.float32) * np.float32(np.sqrt(2.0 / H))
        lora_B = jax.random.normal(ks[6], (E, H, LORA_R), dtype=jnp.float32) * np.float32(np.sqrt(2.0 / LORA_R))
        return {'x': x, 'G': G, 'gate_w': gate_w, 'up_w': up_w, 'down_w': down_w, 'lora_A': lora_A, 'lora_B': lora_B}
    _L0_ffn_all = _L0_ffn_setup()
    _L0_ffn_in = {k: v for k, v in _L0_ffn_all.items() if k in ('G', 'gate_w', 'up_w', 'down_w', 'lora_A', 'lora_B')}
    del _L0_ffn_all
    return {'x': x, 'itok_BxS_13_99985': itok_BxS_13_99985, 'ctx_2048': ctx_2048, 'L0_ffn_G': _L0_ffn_in['G'], 'L0_ffn_gate_w': _L0_ffn_in['gate_w'], 'L0_ffn_up_w': _L0_ffn_in['up_w'], 'L0_ffn_down_w': _L0_ffn_in['down_w'], 'L0_ffn_lora_A': _L0_ffn_in['lora_A'], 'L0_ffn_lora_B': _L0_ffn_in['lora_B']}

def reference(x, itok_BxS_13_99985, ctx_2048, L0_ffn_G, L0_ffn_gate_w, L0_ffn_up_w, L0_ffn_down_w, L0_ffn_lora_A, L0_ffn_lora_B):
    import jax
    import jax.numpy as jnp

    def _L0_xattn_ref(hidden_states, token_ids, Wg, Wu, Wd):
        import jax, jax.numpy as jnp
        import numpy as np
        B, S, D = (4, 1024, 512)
        E = 4
        F = 2048 // E
        VOCAB = 25000
        tokens_per_expert = VOCAB // E
        tid = jnp.clip(token_ids, 0, VOCAB - 1)
        expert_ids = jnp.minimum(tid // tokens_per_expert, E - 1)
        out = jnp.zeros_like(hidden_states)
        for e in range(E):
            g = jax.nn.silu(jnp.einsum('bsd,fd->bsf', hidden_states, Wg[e]))
            u = jnp.einsum('bsd,fd->bsf', hidden_states, Wu[e])
            y = jnp.einsum('bsf,df->bsd', g * u, Wd[e])
            out = jnp.where((expert_ids == e)[..., None], y, out)
        return out

    def _L0_ffn_ref(x, G, gate_w, up_w, down_w, lora_A, lora_B):
        import jax, jax.numpy as jnp
        import numpy as np
        B, S, H = (4, 512, 512)
        E = 8
        F = H // E
        TOPK = 2
        LORA_R = 16
        LORA_SCALE = 1.0
        scores = jax.nn.softmax(jnp.einsum('bsh,he->bse', x, G), axis=-1)
        value, indices = jax.lax.top_k(scores, TOPK)
        onehot = jax.nn.one_hot(indices, E, dtype=value.dtype)
        w = jnp.einsum('bsk,bske->bse', value, onehot)
        gate = jax.nn.silu(jnp.einsum('bsh,efh->bsef', x, gate_w))
        up = jnp.einsum('bsh,efh->bsef', x, up_w)
        gated = gate * up
        out = jnp.einsum('bsef,bse,ehf->bsh', gated, w, down_w)
        lr = jnp.einsum('bsh,erh->bser', x, lora_A)
        out = out + LORA_SCALE * jnp.einsum('bser,bse,ehr->bsh', lr, w, lora_B)
        return out
    x = x + _L0_xattn_ref(_layernorm(x, axis=-1), itok_BxS_13_99985, ctx_2048, ctx_2048, ctx_2048)
    x = x + _L0_ffn_ref(_layernorm(x, axis=-1), L0_ffn_G, L0_ffn_gate_w, L0_ffn_up_w, L0_ffn_down_w, L0_ffn_lora_A, L0_ffn_lora_B)
    return x

_drawn_inputs = setup_inputs


def setup_inputs(seed=0):
    import zlib

    import numpy as np

    out = dict(_drawn_inputs(seed))
    spreads = {}
    factors = {}
    for name, (base, spread) in spreads.items():
        noise = np.random.default_rng([zlib.crc32(name.encode()), seed]).standard_normal(out[name].shape)
        drawn = base * np.exp(spread * noise) if base else spread * noise
        out[name] = jnp.asarray(drawn.astype(out[name].dtype))
    for name, factor in factors.items():
        out[name] = (out[name] * factor).astype(out[name].dtype)
    return out
```

```python
from contextlib import ExitStack

import concourse.bass as bass
from concourse import mybir

F32 = mybir.dt.float32
F32R = mybir.dt.float32r
F16 = mybir.dt.float16
I32 = mybir.dt.int32
U32 = mybir.dt.uint32
ALU = mybir.AluOpType
ACT = mybir.ActivationFunctionType
AX_X = mybir.AxisListType.X

P = 128
D = 512
KB = D // P
TOKENS = 4 * 512
TILES = TOKENS // P
E1, VOCAB = 4, 25000
STEPS = TILES + E1 - 1
ROWS = STEPS + TILES
E2, FE, LR = 8, 64, 16
HID = E2 * FE
LORA = E2 * LR
ROUTE0 = LORA
GATE0 = LORA + E2
UP0 = GATE0 + HID
UPW = UP0 + HID
DN = HID + LORA
DB = DN // P
EPS = 1e-5
COMPACT0 = 64
XRING = 8
CTX = KB * D
W2 = KB * UPW + DB * D
DOWN0 = KB * UPW
PIECES = 15
PIECE = W2 // PIECES


def build(nc, x, token_ids, ctx_t, w_up, w_down, out):
    x1_rows = nc.dram_tensor("x1_rows", [TOKENS + STEPS * P, D], F32, kind="Internal").ap()

    with ExitStack() as stack:
        def sb(name, shape, dt=F32):
            return stack.enter_context(nc.sbuf_tensor(name, shape, dt))

        def ps(name, cols):
            return stack.enter_context(nc.psum_tensor(name, [P, cols], F32))

        def sem(name):
            return stack.enter_context(nc.semaphore(name))

        stage = sb("stage", [P, E1 * CTX])
        ctx_hi, ctx_lo = (sb(n, [P, E1 * KB, D], F32R) for n in ("ctx_hi", "ctx_lo"))
        w2_hi, w2_lo = (sb(n, [P, W2], F32R) for n in ("w2_hi", "w2_lo"))
        xin = sb("xin", [P, XRING, D])
        xn = sb("xn", [P, 2, D])
        xT_hi, xT_lo = (sb(n, [P, KB * P], F32R) for n in ("xT_hi", "xT_lo"))
        silu = sb("silu", [P, D])
        upped = sb("upped", [P, HID])
        act = sb("act", [P, DN])
        aT_hi, aT_lo = (sb(n, [P, DB * P], F32R) for n in ("aT_hi", "aT_lo"))
        xout = sb("xout", [P, 2, D])
        bn6 = sb("bn6", [P, 2, 6])
        mean_var = sb("mean_var", [P, 2, 2])
        var_eps = sb("var_eps", [P, 2])
        rstd = sb("rstd", [P, 2])
        neg_half = sb("neg_half", [P, 1])
        logits = sb("logits", [P, E2])
        top1, top8 = sb("top1", [P, 1]), sb("top8", [P, 8])
        top8_at = sb("top8_at", [P, 8], U32)
        chosen1, chosen = sb("chosen1", [P, E2]), sb("chosen", [P, E2])
        z, z_silu, z_rest, z_rest_inv, z_exp, gates = (
            sb(n, [P, E2]) for n in ("z", "z_silu", "z_rest", "z_rest_inv", "z_exp", "gates"))
        z_sum, z_sum_inv = sb("z_sum", [P, 1]), sb("z_sum_inv", [P, 1])
        col = sb("col", [P, P], I32)
        part = sb("part", [P, 1], I32)
        token = sb("token", [P, TILES], I32)
        pad_row = sb("pad_row", [P, STEPS], I32)
        ident = sb("ident", [P, P])
        below = sb("below", [P, P])
        ones = sb("ones", [P, P])
        ids = sb("ids", [P, TILES], I32)
        from_e = sb("from_e", [P, E1 + 1, TILES])
        is_e = sb("is_e", [P, E1, TILES])
        carry = sb("carry", [P, E1, TILES])
        upto, before = sb("upto", [P, E1, TILES]), sb("before", [P, E1, TILES])
        totals = sb("totals", [P, 2, E1])
        counts = sb("counts", [P, E1])
        tiles_i = sb("tiles_i", [P, E1], I32)
        tot_before = sb("tot_before", [P, 2, E1])
        first = sb("first", [P, 2, E1])
        slot_e = sb("slot_e", [P, 2, E1, TILES])
        slot_f = sb("slot_f", [P, 2, TILES])
        slot = sb("slot", [P, 2, TILES], I32)
        slot_lo, slot_hi = sb("slot_lo", [P, 2, TILES], I32), sb("slot_hi", [P, 2, TILES], I32)
        in_lo = [b[:].rearrange("p a d -> p (a d)").bitcast(F16).rearrange("p (c q) -> p c q", q=P) for b in (xout, xn)]
        in_tile = sb("in_tile", [P, TILES, TILES], F16)
        put_padded = sb("put_padded", [P, TILES, 3, STEPS], F16)
        put_compact = sb("put_compact", [P, TILES, TILES], F16)
        empty = sb("empty", [P, STEPS])
        empty_row = sb("empty_row", [P, STEPS])
        gather_row = sb("gather_row", [P, STEPS], U32)
        x1_row = sb("x1_row", [P, STEPS], U32)
        out_row = sb("out_row", [P, TILES], U32)
        step_ge = sb("step_ge", [1, 2, STEPS])
        step_expert = sb("step_expert", [1, STEPS], I32)

        p_xT, p_h, p_up, p_route, p_y = (ps(n, 512) for n in ("p_xT", "p_h", "p_up", "p_route", "p_y"))
        p_aT = ps("p_aT", 1024)
        p_sort = ps("p_sort", 512)

        ids_landed, up_landed, down_landed = sem("ids_landed"), sem("up_landed"), sem("down_landed")
        ctx_landed = [sem(f"ctx_landed{e}") for e in range(E1)]
        iotas_ready, sort_step, masks_ready = sem("iotas_ready"), sem("sort_step"), sem("masks_ready")
        counts_ready, offsets_ready = sem("counts_ready"), sem("offsets_ready")
        onehots_ready, slots_ready, rows_ready = sem("onehots_ready"), sem("slots_ready"), sem("rows_ready")
        half_ready = sem("half_ready")
        ctx_hi_ready, ctx_lo_ready = sem("ctx_hi_ready"), sem("ctx_lo_ready")
        w2_hi_ready, w2_lo_ready = sem("w2_hi_ready"), sem("w2_lo_ready")
        x_landed = [sem("x_landed0"), sem("x_landed1")]
        x1_landed = [sem("x1_landed0"), sem("x1_landed1")]
        bn6_ready, mean_ready, var_ready = sem("bn6_ready"), sem("mean_ready"), sem("var_ready")
        rstd_ready, xn_ready, xT_ready = sem("rstd_ready"), sem("xn_ready"), sem("xT_ready")
        xhi_ready, xlo_ready = sem("xhi_ready"), sem("xlo_ready")
        silu_ready, act_ready, aT_ready = sem("silu_ready"), sem("act_ready"), sem("aT_ready")
        ahi_ready, alo_ready = sem("ahi_ready"), sem("alo_ready")
        y_ready, xout_ready = sem("y_ready"), sem("xout_ready")
        stored = [sem("stored0"), sem("stored1")]
        h_ready = sem("h_ready")
        route_ready, gate_ready, up_ready = sem("route_ready"), sem("gate_ready"), sem("up_ready")
        z_ready, z_silu_ready = sem("z_ready"), sem("z_silu_ready")
        router_step, upped_ready = sem("router_step"), sem("upped_ready")

        block = stack.enter_context(nc.Block())

        def pair(h, c):
            return 2 * h + c, h + c // 2, c % 2

        def one(r):
            return r, r // 2, r % 2

        def x_rows_of(r):
            return xin[:, bass.ds(r % XRING, 1), :].rearrange("p a d -> p (a d)")

        @block.sync
        def _(sp):
            sp.dma_start(ids[:], token_ids).then_inc(ids_landed, 16)
            for e in range(E1):
                sp.dma_start(stage[:, e * CTX:(e + 1) * CTX], ctx_t[:, e, :]).then_inc(ctx_landed[e], 16)
            sp.wait_ge(ctx_lo_ready, E1)
            sp.dma_start(stage[:, 0:DOWN0], w_up).then_inc(up_landed, 16)
            sp.dma_start(stage[:, DOWN0:W2], w_down).then_inc(down_landed, 16)
            for t in range(TILES):
                r = STEPS + t
                sp.wait_ge(stored[0], 16 * ((t + 3) // 2 + 1))
                sp.wait_ge(stored[1], 16 * ((t + 4) // 2))
                sp.wait_ge(xout_ready, r - XRING + 1)
                if t >= 2:
                    sp.wait_ge(x1_landed[t % 2], 16 * (t // 2))
                sp.dma_start(xin[:, r % XRING, :], x1_rows[t * P:(t + 1) * P, :]).then_inc(x1_landed[t % 2], 16)

        @block.gpsimd
        def _(pool):
            nc.gpsimd.iota(col[:], [[1, P]], base=0, channel_multiplier=0).then_inc(iotas_ready, 1)
            nc.gpsimd.iota(part[:], [[1, 1]], base=0, channel_multiplier=1).then_inc(iotas_ready, 1)
            nc.gpsimd.iota(token[:], [[1, TILES]], base=0, channel_multiplier=TILES).then_inc(iotas_ready, 1)
            nc.gpsimd.iota(pad_row[:], [[P, STEPS]], base=TOKENS, channel_multiplier=1).then_inc(iotas_ready, 1)
            nc.gpsimd.memset(neg_half[:], -0.5).then_inc(half_ready, 1)
            pool.wait_ge(half_ready, 1)

            def gather(r):
                if r >= XRING:
                    pool.wait_ge(xout_ready, r - XRING + 1)
                if r >= 2:
                    pool.wait_ge(x_landed[r % 2], 16 * (r // 2))
                nc.gpsimd.indirect_dma_start(
                    out=xin[:, r % XRING, :], out_offset=None, in_=x,
                    in_offset=bass.IndirectOffsetOnAxis(ap=gather_row[:, r:r + 1], axis=0),
                ).then_inc(x_landed[r % 2], 16)

            def inverse_deviation(r):
                pool.wait_ge(var_ready, r + 1)
                nc.gpsimd.tensor_tensor(rstd[:, r % 2:r % 2 + 1], var_eps[:, r % 2:r % 2 + 1], neg_half[:],
                                        ALU.pow).then_inc(rstd_ready, 1)

            def store(r):
                pool.wait_ge(xout_ready, r + 1)
                to, rows = (x1_rows, x1_row[:, r:r + 1]) if r < STEPS else (out, out_row[:, r - STEPS:r - STEPS + 1])
                nc.gpsimd.indirect_dma_start(
                    out=to, out_offset=bass.IndirectOffsetOnAxis(ap=rows, axis=0), in_=xout[:, r % 2, :],
                    in_offset=None).then_inc(stored[r % 2], 16)

            def split_lo(n):
                pool.wait_ge(w2_hi_ready, n + 1)
                piece = slice(n * PIECE, (n + 1) * PIECE)
                nc.gpsimd.tensor_tensor(w2_lo[:, piece], stage[:, piece], w2_hi[:, piece].bitcast(F32),
                                        ALU.subtract).then_inc(w2_lo_ready, 1)

            pool.wait_ge(rows_ready, 1)
            for r in range(4):
                gather(r)
            for r in range(3):
                inverse_deviation(r)
            for r in range(4, 6):
                gather(r)
            pool.wait_ge(rows_ready, 3)
            for k in range(ROWS + 2):
                if k >= 2:
                    store(k - 2)
                if k + 3 < ROWS:
                    inverse_deviation(k + 3)
                if k + 6 < STEPS:
                    gather(k + 6)
                if 1 <= k <= PIECES:
                    split_lo(k - 1)
            pool.wait_ge(stored[0], 16 * ((ROWS + 1) // 2))
            pool.wait_ge(stored[1], 16 * (ROWS // 2))

        @block.scalar
        def _(sc):
            for e in range(E1):
                sc.wait_ge(ctx_landed[e], 16)
                nc.scalar.activation(ctx_hi[:, e * KB:(e + 1) * KB, :].rearrange("p k f -> p (k f)"),
                                     stage[:, e * CTX:(e + 1) * CTX], ACT.Copy).then_inc(ctx_hi_ready, 1)

            def hi_x(r):
                sc.wait_ge(xT_ready, r + 1)
                nc.scalar.activation(xT_hi[:], p_xT[:], ACT.Copy).then_inc(xhi_ready, 1)

            def hi_act(r, cols):
                sc.wait_ge(aT_ready, r + 1)
                nc.scalar.activation(aT_hi[:, 0:cols], p_aT[:, 0:cols], ACT.Copy).then_inc(ahi_ready, 1)

            def l1_silu(k):
                sc.wait_ge(h_ready, k + 1)
                nc.scalar.activation(silu[:], p_h[:], ACT.Silu).then_inc(silu_ready, 1)

            def l2_silus(t):
                sc.wait_ge(z_ready, t + 1)
                nc.scalar.activation(z_silu[:], z[:], ACT.Silu).then_inc(z_silu_ready, 1)
                sc.wait_ge(gate_ready, t + 1)
                nc.scalar.activation(silu[:], p_h[:], ACT.Silu).then_inc(silu_ready, 1)

            def split_hi(n):
                piece = bass.ds(n * PIECE, PIECE)
                nc.scalar.activation(w2_hi[:, piece], stage[:, piece], ACT.Copy).then_inc(w2_hi_ready, 1)

            hi_x(0)
            l1_silu(0)
            hi_x(1)
            sc.wait_ge(up_landed, 16)
            sc.wait_ge(down_landed, 16)
            with sc.Fori(1, PIECES + 1) as k:
                hi_act(k - 1, D)
                split_hi(k - 1)
                l1_silu(k)
                hi_x(k + 1)
            with sc.Fori(PIECES + 1, STEPS) as k:
                hi_act(k - 1, D)
                l1_silu(k)
                hi_x(k + 1)
            hi_act(STEPS - 1, D)
            l2_silus(0)
            hi_x(STEPS + 1)
            with sc.Fori(1, TILES - 1) as t:
                hi_act(STEPS + t - 1, DN)
                l2_silus(t)
                hi_x(STEPS + t + 1)
            hi_act(ROWS - 2, DN)
            l2_silus(TILES - 1)
            hi_act(ROWS - 1, DN)

        @block.vector
        def _(dve):
            done = {sort_step: 0}

            def step(ins):
                done[sort_step] += 1
                ins.then_inc(sort_step, 1)
                dve.wait_ge(sort_step, done[sort_step])

            nc.vector.memset(ones[:], 1.0).then_inc(masks_ready, 1)
            nc.vector.memset(from_e[:, 0, :], 1.0)
            nc.vector.memset(from_e[:, E1, :], 0.0)
            nc.vector.memset(carry[:], 1.0)
            dve.wait_ge(iotas_ready, 4)
            nc.vector.tensor_tensor(below[:], col[:], part[:].broadcast_to([P, P]), ALU.is_gt).then_inc(masks_ready, 1)
            step(nc.vector.tensor_tensor(ident[:], col[:], part[:].broadcast_to([P, P]), ALU.is_equal))
            nc.vector.memset(carry[:, :, 0:1], 0.0)
            dve.wait_ge(ids_landed, 16)
            for e in range(1, E1):
                last = nc.vector.tensor_scalar(from_e[:, e, :], ids[:], float(VOCAB // E1 * e), None, ALU.is_ge)
            step(last)
            step(nc.vector.tensor_tensor(is_e[:], from_e[:, 0:E1, :], from_e[:, 1:E1 + 1, :], ALU.subtract))
            flat = "p e c -> p (e c)"
            step(nc.vector.tensor_tensor_scan(upto[:].rearrange(flat), carry[:].rearrange(flat),
                                              is_e[:].rearrange(flat), 0.0, ALU.mult, ALU.add))
            nc.vector.tensor_copy(counts[:], upto[:, :, TILES - 1]).then_inc(counts_ready, 1)
            nc.vector.tensor_tensor(before[:], upto[:], is_e[:], ALU.subtract)
            dve.wait_ge(offsets_ready, 1)
            nc.vector.tensor_copy(totals[:, 0, :], p_sort[:, E1:2 * E1])
            step(nc.vector.tensor_scalar(tiles_i[:], p_sort[:, E1:2 * E1], float(P - 1), None, ALU.add))
            step(nc.vector.tensor_scalar(tiles_i[:], tiles_i[:], P.bit_length() - 1, None, ALU.logical_shift_right))
            step(nc.vector.tensor_copy(totals[:, 1, :], tiles_i[:]))
            nc.vector.memset(tot_before[:, :, 0], 0.0)
            step(nc.vector.tensor_copy(tot_before[:, :, 1], totals[:, :, 0]))
            for e in range(2, E1):
                step(nc.vector.tensor_tensor(tot_before[:, :, e], tot_before[:, :, e - 1], totals[:, :, e - 1], ALU.add))
            nc.vector.tensor_tensor(first[:, 0, :], p_sort[:, 0:E1], tot_before[:, 0, :], ALU.add)
            step(nc.vector.scalar_tensor_tensor(first[:, 1, :], tot_before[:, 1, :], float(P), p_sort[:, 0:E1],
                                                ALU.mult, ALU.add))
            every = [P, 2, E1, TILES]
            step(nc.vector.tensor_tensor(slot_e[:], before[:].unsqueeze(1).broadcast_to(every),
                                         first[:].unsqueeze(3).broadcast_to(every), ALU.add))
            step(nc.vector.tensor_tensor(slot_e[:], slot_e[:], is_e[:].unsqueeze(1).broadcast_to(every), ALU.mult))
            step(nc.vector.tensor_reduce(slot_f[:], slot_e[:].rearrange("p m e c -> p m c e"), AX_X, ALU.add))
            step(nc.vector.tensor_copy(slot[:], slot_f[:]))
            nc.vector.tensor_scalar(slot_lo[:], slot[:], P - 1, None, ALU.bitwise_and)
            step(nc.vector.tensor_scalar(slot_hi[:], slot[:], P.bit_length() - 1, None, ALU.logical_shift_right))
            for m in range(2):
                nc.vector.tensor_tensor(in_lo[m], col[:].unsqueeze(1).broadcast_to([P, TILES, P]),
                                        slot_lo[:, m].unsqueeze(2).broadcast_to([P, TILES, P]), ALU.is_equal)
            to_steps, to_tiles = [P, TILES, STEPS], [P, TILES, TILES]
            nc.vector.tensor_tensor(in_tile[:], col[:, 0:TILES].unsqueeze(1).broadcast_to(to_tiles),
                                    slot_hi[:, 0].unsqueeze(2).broadcast_to(to_tiles), ALU.is_equal)
            step(nc.vector.tensor_tensor(put_padded[:, :, 2], col[:, 0:STEPS].unsqueeze(1).broadcast_to(to_steps),
                                         slot_hi[:, 1].unsqueeze(2).broadcast_to(to_steps), ALU.is_equal))
            nc.vector.tensor_tensor(put_padded[:, :, 0], put_padded[:, :, 2],
                                    token[:].unsqueeze(2).broadcast_to(to_steps), ALU.mult)
            nc.vector.tensor_tensor(put_padded[:, :, 1], put_padded[:, :, 2],
                                    slot[:, 0].unsqueeze(2).broadcast_to(to_steps), ALU.mult)
            nc.vector.tensor_tensor(put_compact[:], in_tile[:], token[:].unsqueeze(2).broadcast_to(to_tiles),
                                    ALU.mult).then_inc(onehots_ready, 1)

            def split_ctx(e):
                dve.wait_ge(ctx_hi_ready, e + 1)
                nc.vector.tensor_tensor(ctx_lo[:, e * KB:(e + 1) * KB, :].rearrange("p k f -> p (k f)"),
                                        stage[:, e * CTX:(e + 1) * CTX],
                                        ctx_hi[:, e * KB:(e + 1) * KB, :].rearrange("p k f -> p (k f)").bitcast(F32),
                                        ALU.subtract).then_inc(ctx_lo_ready, 1)

            split_ctx(0)
            dve.wait_ge(slots_ready, 1)
            nc.vector.tensor_copy(gather_row[:], p_sort[:, 0:STEPS]).then_inc(rows_ready, 1)
            step(nc.vector.tensor_scalar(empty[:], p_sort[:, 2 * STEPS:3 * STEPS], -1.0, 1.0, ALU.mult, ALU.add))
            step(nc.vector.tensor_tensor(empty_row[:], empty[:], pad_row[:], ALU.mult))
            nc.vector.tensor_tensor(x1_row[:], p_sort[:, STEPS:2 * STEPS], empty_row[:], ALU.add).then_inc(rows_ready, 1)
            nc.vector.tensor_copy(out_row[:], p_sort[:, COMPACT0:COMPACT0 + TILES]).then_inc(rows_ready, 1)
            step(nc.vector.tensor_scalar(step_ge[:, 0, :], col[0:1, 0:STEPS], tot_before[0:1, 1, 1:2], None, ALU.is_ge))
            step(nc.vector.scalar_tensor_tensor(step_ge[:, 1, :], col[0:1, 0:STEPS], tot_before[0:1, 1, 2:3],
                                                step_ge[:, 0, :], ALU.is_ge, ALU.add))
            nc.vector.scalar_tensor_tensor(step_expert[:], col[0:1, 0:STEPS], tot_before[0:1, 1, 3:4],
                                           step_ge[:, 1, :], ALU.is_ge, ALU.add).then_inc(rows_ready, 1)
            for e in range(1, E1):
                split_ctx(e)

            def statistics(row, tile=None, between=None):
                r, half, parity = row
                if tile is None:
                    dve.wait_ge(x_landed[parity], 16 * (half + 1))
                else:
                    dve.wait_ge(x1_landed[tile[2]], 16 * (tile[1] + 1))
                nc.vector.bn_stats(bn6[:, parity, :], x_rows_of(r)).then_inc(bn6_ready, 1)
                dve.wait_ge(bn6_ready, r + 1)
                if between is not None:
                    normalise(between)
                nc.vector.bn_aggr(mean_var[:, parity, :], bn6[:, parity, :]).then_inc(mean_ready, 1)
                dve.wait_ge(mean_ready, r + 1)
                nc.vector.tensor_scalar(var_eps[:, parity:parity + 1], mean_var[:, parity, 1:2], EPS, None,
                                        ALU.add).then_inc(var_ready, 1)

            def normalise(row, first_use=False):
                r, _, parity = row
                dve.wait_ge(rstd_ready, r + 1)
                if not first_use:
                    dve.wait_ge(xT_ready, r - 1)
                nc.vector.tensor_scalar(xn[:, parity, :], x_rows_of(r), mean_var[:, parity, 0:1],
                                        rstd[:, parity:parity + 1], ALU.subtract, ALU.mult).then_inc(xn_ready, 1)

            def lo_x(r):
                dve.wait_ge(xhi_ready, r + 1)
                nc.vector.tensor_tensor(xT_lo[:], p_xT[:], xT_hi[:].bitcast(F32), ALU.subtract).then_inc(xlo_ready, 1)

            def lo_act(r, cols):
                dve.wait_ge(ahi_ready, r + 1)
                nc.vector.tensor_tensor(aT_lo[:, 0:cols], p_aT[:, 0:cols], aT_hi[:, 0:cols].bitcast(F32),
                                        ALU.subtract).then_inc(alo_ready, 1)

            def residual(row, first_use=False):
                r, half, parity = row
                dve.wait_ge(y_ready, r + 1)
                if not first_use:
                    dve.wait_ge(stored[parity], 16 * half)
                nc.vector.tensor_tensor(xout[:, parity, :], p_y[:], x_rows_of(r), ALU.add).then_inc(xout_ready, 1)

            def l1_gate(k):
                dve.wait_ge(silu_ready, k + 1)
                nc.vector.tensor_tensor(act[:, 0:D], silu[:], p_h[:], ALU.mult).then_inc(act_ready, 1)

            def l2_gates(t):
                of = 12 * t
                dve.wait_ge(route_ready, t + 1)
                nc.vector.tensor_copy(logits[:], p_route[:, ROUTE0:ROUTE0 + E2]).then_inc(router_step, 1)
                dve.wait_ge(router_step, of + 1)
                nc.vector.tensor_reduce(top1[:], logits[:], AX_X, ALU.max).then_inc(router_step, 1)
                nc.vector.max(top8[:], logits[:]).then_inc(router_step, 1)
                dve.wait_ge(router_step, of + 3)
                nc.vector.tensor_scalar(z[:], logits[:], top1[:, 0:1], -1.0, ALU.subtract, ALU.add).then_inc(z_ready, 1)
                nc.vector.max_index(top8_at[:], top8[:], logits[:]).then_inc(router_step, 1)
                dve.wait_ge(router_step, of + 4)
                nc.vector.tensor_scalar(chosen1[:], col[:, 0:E2], top8_at[:, 0:1], None,
                                        ALU.is_equal).then_inc(router_step, 1)
                dve.wait_ge(router_step, of + 5)
                nc.vector.scalar_tensor_tensor(chosen[:], col[:, 0:E2], top8_at[:, 1:2], chosen1[:],
                                               ALU.is_equal, ALU.add).then_inc(router_step, 1)
                dve.wait_ge(z_silu_ready, t + 1)
                nc.vector.tensor_tensor(z_rest[:], z[:], z_silu[:], ALU.subtract).then_inc(router_step, 1)
                dve.wait_ge(router_step, of + 7)
                nc.vector.reciprocal(z_rest_inv[:], z_rest[:]).then_inc(router_step, 1)
                dve.wait_ge(router_step, of + 8)
                nc.vector.tensor_tensor(z_exp[:], z_silu[:], z_rest_inv[:], ALU.mult).then_inc(router_step, 1)
                dve.wait_ge(router_step, of + 9)
                nc.vector.tensor_reduce(z_sum[:], z_exp[:], AX_X, ALU.add).then_inc(router_step, 1)
                dve.wait_ge(router_step, of + 10)
                nc.vector.reciprocal(z_sum_inv[:], z_sum[:]).then_inc(router_step, 1)
                dve.wait_ge(router_step, of + 11)
                nc.vector.scalar_tensor_tensor(gates[:], z_exp[:], z_sum_inv[:, 0:1], chosen[:],
                                               ALU.mult, ALU.mult).then_inc(router_step, 1)
                dve.wait_ge(router_step, of + 12)

            def l2_act(r, t):
                by_expert = "p (e f) -> p e f"
                nc.vector.tensor_tensor(act[:, HID:DN].rearrange(by_expert, e=E2),
                                        p_route[:, 0:LORA].rearrange(by_expert, e=E2),
                                        gates[:].unsqueeze(2).broadcast_to([P, E2, LR]), ALU.mult)
                dve.wait_ge(silu_ready, r + 1)
                dve.wait_ge(up_ready, t + 1)
                nc.vector.tensor_tensor(upped[:], silu[:], p_up[:], ALU.mult).then_inc(upped_ready, 1)
                dve.wait_ge(upped_ready, t + 1)
                nc.vector.tensor_tensor(act[:, 0:HID].rearrange(by_expert, e=E2),
                                        upped[:].rearrange(by_expert, e=E2),
                                        gates[:].unsqueeze(2).broadcast_to([P, E2, FE]), ALU.mult).then_inc(act_ready, 1)

            for r in range(2):
                statistics(one(r))
            normalise(one(0), first_use=True)
            statistics(one(2))
            normalise(one(1), first_use=True)
            lo_x(0)
            for k in range(4):
                if k >= 1:
                    lo_act(k - 1, D)
                if k >= 2:
                    residual(one(k - 2), first_use=True)
                statistics(one(k + 3), between=one(k + 2))
                l1_gate(k)
                lo_x(k + 1)
            with dve.Fori(2, (STEPS - 3) // 2) as h:
                for u in range(2):
                    k = 2 * h + u
                    lo_act(k - 1, D)
                    residual(pair(h, u - 2))
                    statistics(pair(h, u + 3), between=pair(h, u + 2))
                    l1_gate(k)
                    lo_x(k + 1)
            for k in range(STEPS - 3, STEPS):
                lo_act(k - 1, D)
                residual(one(k - 2))
                statistics(one(k + 3), tile=one(k + 3 - STEPS), between=one(k + 2))
                l1_gate(k)
                lo_x(k + 1)

            r = STEPS
            lo_act(r - 1, D)
            residual(one(r - 2))
            statistics(one(r + 3), tile=one(3), between=one(r + 2))
            l2_gates(0)
            l2_act(r, 0)
            lo_x(r + 1)
            with dve.Fori(0, (TILES - 4) // 2) as h:
                for u in range(2):
                    t = 2 * h + u + 1
                    c = STEPS + 1 + u
                    lo_act(2 * h + c - 1, DN)
                    residual(pair(h, c - 2))
                    statistics(pair(h, c + 3), tile=pair(h, u + 4), between=pair(h, c + 2))
                    l2_gates(t)
                    l2_act(2 * h + c, t)
                    lo_x(2 * h + c + 1)
            for t in range(TILES - 3, TILES):
                r = STEPS + t
                lo_act(r - 1, DN)
                residual(one(r - 2))
                if r + 2 < ROWS:
                    normalise(one(r + 2))
                l2_gates(t)
                l2_act(r, t)
                if r + 1 < ROWS:
                    lo_x(r + 1)
            lo_act(ROWS - 1, DN)
            residual(one(ROWS - 2))
            residual(one(ROWS - 1))

        @block.tensor
        def _(pe):
            pe.wait_ge(masks_ready, 2)
            pe.wait_ge(counts_ready, 1)
            nc.tensor.matmul(p_sort[:, 0:E1], below[:], counts[:], start=True, stop=True)
            nc.tensor.matmul(p_sort[:, E1:2 * E1], ones[:], counts[:], start=True, stop=True).then_inc(offsets_ready, 1)
            pe.wait_ge(onehots_ready, 1)
            for c in range(TILES):
                nc.tensor.matmul(p_sort[:, 0:3 * STEPS], in_lo[1][:, c, :], put_padded[:, c].rearrange("p v s -> p (v s)"),
                                 start=(c == 0), stop=(c == TILES - 1))
            for c in range(TILES):
                last = nc.tensor.matmul(p_sort[:, COMPACT0:COMPACT0 + TILES], in_lo[0][:, c, :], put_compact[:, c, :],
                                        start=(c == 0), stop=(c == TILES - 1))
            last.then_inc(slots_ready, 1)

            def blk(i):
                return slice(i * P, (i + 1) * P)

            def turn_x(r, parity):
                pe.wait_ge(xn_ready, r + 1)
                for i in range(KB):
                    last = nc.tensor.transpose(p_xT[:, blk(i)], xn[:, parity, blk(i)], ident[:])
                last.then_inc(xT_ready, 1)

            def turn_act(r, blocks):
                pe.wait_ge(act_ready, r + 1)
                for i in range(blocks):
                    last = nc.tensor.transpose(p_aT[:, blk(i)], act[:, blk(i)], ident[:])
                last.then_inc(aT_ready, 1)

            def product(to, hi, lo, blocks, w_hi, w_lo):
                for i in range(blocks):
                    nc.tensor.matmul(to, hi[:, blk(i)], w_hi(i), start=(i == 0), stop=False)
                    nc.tensor.matmul(to, hi[:, blk(i)], w_lo(i), start=False, stop=False)
                for i in range(blocks):
                    last = nc.tensor.matmul(to, lo[:, blk(i)], w_hi(i), start=False, stop=(i == blocks - 1))
                return last

            def l1_matrix(k):
                e = pe.value_load(step_expert[0:1, bass.ds(k, 1)], min_val=0, max_val=E1 - 1)
                return [lambda i, w=w: w[:, bass.ds(e * KB + i, 1), :].rearrange("p a f -> p (a f)")
                        for w in (ctx_hi, ctx_lo)]

            def l1_first(k):
                w = l1_matrix(k)
                pe.wait_ge(xhi_ready, k + 1)
                pe.wait_ge(xlo_ready, k + 1)
                product(p_h[:], xT_hi, xT_lo, KB, *w).then_inc(h_ready, 1)

            def l1_second(k, first_use=False):
                w = l1_matrix(k)
                pe.wait_ge(ahi_ready, k + 1)
                pe.wait_ge(alo_ready, k + 1)
                if not first_use:
                    pe.wait_ge(xout_ready, k)
                product(p_y[:], aT_hi, aT_lo, KB, *w).then_inc(y_ready, 1)

            def up_part(c0, c1):
                return [lambda i, w=w: w[:, i * UPW + c0:i * UPW + c1] for w in (w2_hi, w2_lo)]

            def l2_first(r):
                pe.wait_ge(xhi_ready, r + 1)
                pe.wait_ge(xlo_ready, r + 1)
                for to, c0, c1, ready in ((p_route, 0, GATE0, route_ready), (p_h, GATE0, UP0, gate_ready),
                                          (p_up, UP0, UPW, up_ready)):
                    product(to[:, 0:c1 - c0], xT_hi, xT_lo, KB, *up_part(c0, c1)).then_inc(ready, 1)

            def l2_second(r):
                pe.wait_ge(ahi_ready, r + 1)
                pe.wait_ge(alo_ready, r + 1)
                pe.wait_ge(xout_ready, r)
                product(p_y[:], aT_hi, aT_lo, DB,
                        *[lambda i, w=w: w[:, DOWN0 + i * D:DOWN0 + (i + 1) * D] for w in (w2_hi, w2_lo)]
                        ).then_inc(y_ready, 1)

            pe.wait_ge(rows_ready, 4)
            pe.wait_ge(ctx_lo_ready, E1)
            turn_x(0, 0)
            l1_first(0)
            turn_x(1, 1)
            for k in range(1, 3):
                turn_act(k - 1, KB)
                l1_first(k)
                turn_x(k + 1, (k + 1) % 2)
                l1_second(k - 1, first_use=(k == 1))
            with pe.Fori(1, (STEPS - 1) // 2) as h:
                for u in range(1, 3):
                    k = 2 * h + u
                    turn_act(k - 1, KB)
                    l1_first(k)
                    turn_x(k + 1, (u + 1) % 2)
                    l1_second(k - 1)
            pe.wait_ge(w2_lo_ready, PIECES)
            turn_act(STEPS - 1, KB)
            l2_first(STEPS)
            turn_x(STEPS + 1, (STEPS + 1) % 2)
            l1_second(STEPS - 1)
            with pe.Fori(0, (TILES - 2) // 2) as h:
                for u in range(2):
                    r = 2 * h + STEPS + 1 + u
                    turn_act(r - 1, DB)
                    l2_first(r)
                    turn_x(r + 1, (STEPS + 2 + u) % 2)
                    l2_second(r - 1)
            turn_act(ROWS - 2, DB)
            l2_first(ROWS - 1)
            l2_second(ROWS - 2)
            turn_act(ROWS - 1, DB)
            l2_second(ROWS - 1)


def kernel(x, itok_BxS_13_99985, ctx_2048, L0_ffn_G, L0_ffn_gate_w, L0_ffn_up_w, L0_ffn_down_w, L0_ffn_lora_A,
           L0_ffn_lora_B):
    import numpy as np
    import concourse.bacc as bacc
    from concourse.bass_utils import run_bass_kernel_spmd

    def blocks(m):
        return np.ascontiguousarray(m.reshape(-1, P, m.shape[-1]).transpose(1, 0, 2)).reshape(P, -1)

    ctx = np.asarray(ctx_2048)
    gate, up, lora_a = (np.asarray(a).reshape(-1, D).T for a in (L0_ffn_gate_w, L0_ffn_up_w, L0_ffn_lora_A))
    down, lora_b = (np.asarray(a).transpose(0, 2, 1).reshape(-1, D) for a in (L0_ffn_down_w, L0_ffn_lora_B))
    arrays = {
        "x": np.ascontiguousarray(np.asarray(x).reshape(TOKENS, D)),
        "token_ids": np.ascontiguousarray(np.asarray(itok_BxS_13_99985).reshape(P, TILES)),
        "ctx_t": np.ascontiguousarray(ctx.transpose(0, 2, 1).reshape(E1, KB, P, D).transpose(2, 0, 1, 3)).reshape(P, E1, CTX),
        "w_up": blocks(np.concatenate([lora_a, np.asarray(L0_ffn_G), gate, up], axis=1)),
        "w_down": blocks(np.concatenate([down, lora_b], axis=0)),
    }
    nc = bacc.Bacc("TRN2", target_bir_lowering=False, num_devices=1)
    args = [nc.dram_tensor(n, a.shape, mybir.dt.from_np(a.dtype), kind="ExternalInput").ap() for n, a in arrays.items()]
    out = nc.dram_tensor("out", [TOKENS, D], F32, kind="ExternalOutput").ap()
    build(nc, *args, out)
    result = run_bass_kernel_spmd(nc, [arrays], core_ids=[0])
    return result.results[0]["out"].reshape(4, 512, D)
```

```python
from contextlib import ExitStack

import concourse.bass as bass
from concourse import mybir

F32 = mybir.dt.float32
F32R = mybir.dt.float32r
F16 = mybir.dt.float16
I32 = mybir.dt.int32
U32 = mybir.dt.uint32
ALU = mybir.AluOpType
ACT = mybir.ActivationFunctionType
AX_X = mybir.AxisListType.X

P = 128
D = 512
KB = D // P
TOKENS = 4 * 512
TILES = TOKENS // P
E1, VOCAB = 4, 25000
STEPS = TILES + E1 - 1
ROWS = STEPS + TILES
E2, FE, LR = 8, 64, 16
HID = E2 * FE
LORA = E2 * LR
ROUTE0 = LORA
UP_A0 = LORA + E2
GATE_B0 = UP_A0 + HID // 2
UP_B0 = GATE_B0 + 2 * FE
GATE_C0 = UP_B0 + HID // 2
GATED_B = HID - 2 * FE
UPW = GATE_C0 + GATED_B
DN = HID + LORA
DB = DN // P
EPS = 1e-5
COMPACT0 = 64
XRING = 8
CTX = KB * D
HALF = CTX // 2
W2 = KB * UPW + DB * D
DOWN0 = KB * UPW
PIECES = 15
PIECE = W2 // PIECES
SPLIT0 = 2
UP_PIECES = DOWN0 // PIECE


def build(nc, x, token_ids, ctx_t, w_up, w_down, out):
    x1_rows = nc.dram_tensor("x1_rows", [TOKENS + STEPS * P, D], F32, kind="Internal").ap()

    with ExitStack() as stack:
        def sb(name, shape, dt=F32):
            return stack.enter_context(nc.sbuf_tensor(name, shape, dt))

        def ps(name, cols):
            return stack.enter_context(nc.psum_tensor(name, [P, cols], F32))

        def sem(name):
            return stack.enter_context(nc.semaphore(name))

        stage = sb("stage", [P, E1 * CTX])
        ctx_hi, ctx_lo = (sb(n, [P, E1 * KB, D], F32R) for n in ("ctx_hi", "ctx_lo"))
        w2_hi, w2_lo = (sb(n, [P, W2], F32R) for n in ("w2_hi", "w2_lo"))
        xin = sb("xin", [P, XRING, D])
        xn = sb("xn", [P, 2, D])
        xT_hi, xT_lo = (sb(n, [P, KB * P], F32R) for n in ("xT_hi", "xT_lo"))
        silu = sb("silu", [P, D])
        up_gated = sb("up_gated", [P, HID])
        act = sb("act", [P, DN])
        aT_hi, aT_lo = (sb(n, [P, DB * P], F32R) for n in ("aT_hi", "aT_lo"))
        xout = sb("xout", [P, 2, D])
        bn6 = sb("bn6", [P, 2, 6])
        mean_var = sb("mean_var", [P, 2, 2])
        var_eps = sb("var_eps", [P, 2])
        rstd = sb("rstd", [P, 2])
        neg_half = sb("neg_half", [P, 1])
        logits = sb("logits", [P, E2])
        top1, top8 = sb("top1", [P, 1]), sb("top8", [P, 8])
        top8_at = sb("top8_at", [P, 8], U32)
        chosen1, chosen = sb("chosen1", [P, E2]), sb("chosen", [P, E2])
        z, z_silu, z_rest, z_rest_inv, z_exp, gates = (
            sb(n, [P, E2]) for n in ("z", "z_silu", "z_rest", "z_rest_inv", "z_exp", "gates"))
        z_sum, z_sum_inv = sb("z_sum", [P, 1]), sb("z_sum_inv", [P, 1])
        col = sb("col", [P, P], I32)
        part = sb("part", [P, 1], I32)
        token = sb("token", [P, TILES], I32)
        token_f = sb("token_f", [P, TILES])
        table_warm = sb("table_warm", [P, 1])
        pad_row = sb("pad_row", [P, STEPS], I32)
        ident = sb("ident", [P, P])
        below = sb("below", [P, P])
        ones = sb("ones", [P, P])
        ids = sb("ids", [P, TILES], I32)
        from_e = sb("from_e", [P, E1 + 1, TILES])
        is_e = sb("is_e", [P, E1, TILES])
        carry = sb("carry", [P, E1, TILES])
        upto, before = sb("upto", [P, E1, TILES]), sb("before", [P, E1, TILES])
        totals = sb("totals", [P, 2, E1])
        counts = sb("counts", [P, E1])
        tiles_i = sb("tiles_i", [P, E1], I32)
        tot_before = sb("tot_before", [P, 2, E1])
        first = sb("first", [P, 2, E1])
        slot_e = sb("slot_e", [P, 2, E1, TILES])
        slot_f = sb("slot_f", [P, 2, TILES])
        slot = sb("slot", [P, 2, TILES], I32)
        slot_lo, slot_hi = sb("slot_lo", [P, 2, TILES], I32), sb("slot_hi", [P, 2, TILES], I32)
        in_lo = [b[:].rearrange("p a d -> p (a d)").bitcast(F16).rearrange("p (c q) -> p c q", q=P) for b in (xout, xn)]
        in_tile = sb("in_tile", [P, TILES, TILES], F16)
        put_padded = sb("put_padded", [P, TILES, 3, STEPS], F16)
        put_compact = sb("put_compact", [P, TILES, TILES], F16)
        empty = sb("empty", [P, STEPS])
        empty_row = sb("empty_row", [P, STEPS])
        gather_row = sb("gather_row", [P, STEPS], U32)
        x1_row = sb("x1_row", [P, STEPS], U32)
        out_row = sb("out_row", [P, TILES], U32)
        step_ge = sb("step_ge", [1, 2, STEPS])
        step_expert = sb("step_expert", [1, STEPS], I32)

        p_xT, p_h, p_a, p_b, p_y = (ps(n, 512) for n in ("p_xT", "p_h", "p_a", "p_b", "p_y"))
        p_aT = ps("p_aT", 1024)
        p_sort = ps("p_sort", 512)

        ids_landed, up_landed, down_landed = sem("ids_landed"), sem("up_landed"), sem("down_landed")
        ctx_landed = [sem(f"ctx_landed{e}") for e in range(E1)]
        iotas_ready, sort_step, masks_ready = sem("iotas_ready"), sem("sort_step"), sem("masks_ready")
        counts_ready, offsets_ready = sem("counts_ready"), sem("offsets_ready")
        owners_ready, puts_ready, onehots_ready = sem("owners_ready"), sem("puts_ready"), sem("onehots_ready")
        slots_ready, rows_ready = sem("slots_ready"), sem("rows_ready")
        half_ready = sem("half_ready")
        ctx_hi_ready, ctx_lo_ready = sem("ctx_hi_ready"), sem("ctx_lo_ready")
        w2_hi_ready, w2_lo_ready = sem("w2_hi_ready"), sem("w2_lo_ready")
        x_landed = [sem("x_landed0"), sem("x_landed1")]
        x1_landed = [sem("x1_landed0"), sem("x1_landed1")]
        bn6_ready, mean_ready, var_ready = sem("bn6_ready"), sem("mean_ready"), sem("var_ready")
        rstd_ready, xn_ready, xT_ready = sem("rstd_ready"), sem("xn_ready"), sem("xT_ready")
        xhi_ready, xlo_ready = sem("xhi_ready"), sem("xlo_ready")
        silu_ready, act_ready, aT_ready = sem("silu_ready"), sem("act_ready"), sem("aT_ready")
        ahi_ready, alo_ready = sem("ahi_ready"), sem("alo_ready")
        y_ready, xout_ready = sem("y_ready"), sem("xout_ready")
        stored = [sem("stored0"), sem("stored1")]
        h_ready = sem("h_ready")
        part_a_ready, part_b_ready, part_c_ready = sem("part_a_ready"), sem("part_b_ready"), sem("part_c_ready")
        silu_b_ready, up_gated_ready = sem("silu_b_ready"), sem("up_gated_ready")
        z_ready, z_silu_ready = sem("z_ready"), sem("z_silu_ready")
        router_step = sem("router_step")

        block = stack.enter_context(nc.Block())

        def pair(h, c):
            return 2 * h + c, h + c // 2, c % 2

        def one(r):
            return r, r // 2, r % 2

        def x_rows_of(r):
            return xin[:, bass.ds(r % XRING, 1), :].rearrange("p a d -> p (a d)")

        @block.sync
        def _(sp):
            sp.dma_start(ids[:], token_ids).then_inc(ids_landed, 16)
            for e in range(E1):
                sp.dma_start(stage[:, e * CTX:(e + 1) * CTX], ctx_t[:, e, :]).then_inc(ctx_landed[e], 16)
            sp.wait_ge(ctx_lo_ready, 2 * -(-DOWN0 // CTX))
            sp.dma_start(stage[:, 0:DOWN0], w_up).then_inc(up_landed, 16)
            sp.wait_ge(ctx_lo_ready, 2 * E1)
            sp.dma_start(stage[:, DOWN0:W2], w_down).then_inc(down_landed, 16)
            for t in range(TILES):
                r = STEPS + t
                sp.wait_ge(stored[0], 16 * ((t + 3) // 2 + 1))
                sp.wait_ge(stored[1], 16 * ((t + 4) // 2))
                sp.wait_ge(xout_ready, r - XRING + 1)
                if t >= 2:
                    sp.wait_ge(x1_landed[t % 2], 16 * (t // 2))
                sp.dma_start(xin[:, r % XRING, :], x1_rows[t * P:(t + 1) * P, :]).then_inc(x1_landed[t % 2], 16)

        @block.gpsimd
        def _(pool):
            nc.gpsimd.memset(neg_half[:], -0.5).then_inc(half_ready, 1)
            nc.gpsimd.iota(col[:], [[1, P]], base=0, channel_multiplier=0).then_inc(iotas_ready, 1)
            nc.gpsimd.iota(part[:], [[1, 1]], base=0, channel_multiplier=1).then_inc(iotas_ready, 1)
            nc.gpsimd.iota(token[:], [[1, TILES]], base=0, channel_multiplier=TILES).then_inc(iotas_ready, 1)
            nc.gpsimd.iota(pad_row[:], [[P, STEPS]], base=TOKENS, channel_multiplier=1).then_inc(iotas_ready, 1)
            pool.wait_ge(half_ready, 1)

            def gather(r):
                if r >= XRING:
                    pool.wait_ge(xout_ready, r - XRING + 1)
                if r >= 2:
                    pool.wait_ge(x_landed[r % 2], 16 * (r // 2))
                nc.gpsimd.indirect_dma_start(
                    out=xin[:, r % XRING, :], out_offset=None, in_=x,
                    in_offset=bass.IndirectOffsetOnAxis(ap=gather_row[:, r:r + 1], axis=0),
                ).then_inc(x_landed[r % 2], 16)

            def inverse_deviation(r):
                pool.wait_ge(var_ready, r + 1)
                nc.gpsimd.tensor_tensor(rstd[:, r % 2:r % 2 + 1], var_eps[:, r % 2:r % 2 + 1], neg_half[:],
                                        ALU.pow).then_inc(rstd_ready, 1)

            def store(r):
                pool.wait_ge(xout_ready, r + 1)
                to, rows = (x1_rows, x1_row[:, r:r + 1]) if r < STEPS else (out, out_row[:, r - STEPS:r - STEPS + 1])
                nc.gpsimd.indirect_dma_start(
                    out=to, out_offset=bass.IndirectOffsetOnAxis(ap=rows, axis=0), in_=xout[:, r % 2, :],
                    in_offset=None).then_inc(stored[r % 2], 16)

            def split_lo(n):
                pool.wait_ge(w2_hi_ready, n + 1)
                piece = slice(n * PIECE, (n + 1) * PIECE)
                nc.gpsimd.tensor_tensor(w2_lo[:, piece], stage[:, piece], w2_hi[:, piece].bitcast(F32),
                                        ALU.subtract).then_inc(w2_lo_ready, 1)

            to_steps = [P, TILES, STEPS]
            pool.wait_ge(owners_ready, 1)
            nc.gpsimd.tensor_tensor(put_padded[:, :, 0], put_padded[:, :, 2],
                                    token_f[:].unsqueeze(2).broadcast_to(to_steps), ALU.mult).then_inc(puts_ready, 1)
            nc.gpsimd.tensor_tensor(put_padded[:, :, 1], put_padded[:, :, 2],
                                    slot_f[:, 0].unsqueeze(2).broadcast_to(to_steps), ALU.mult).then_inc(puts_ready, 1)
            pool.wait_ge(rows_ready, 2)
            gather(0)
            gather(1)
            for r in range(3):
                inverse_deviation(r)
                gather(r + 2)
            gather(5)
            pool.wait_ge(rows_ready, 3)
            for k in range(ROWS + 2):
                if k - 2 == STEPS:
                    pool.wait_ge(rows_ready, 4)
                if k >= 2:
                    store(k - 2)
                if k + 3 < ROWS:
                    inverse_deviation(k + 3)
                if k + 6 < STEPS:
                    gather(k + 6)
                if SPLIT0 <= k < SPLIT0 + PIECES:
                    split_lo(k - SPLIT0)
            pool.wait_ge(stored[0], 16 * ((ROWS + 1) // 2))
            pool.wait_ge(stored[1], 16 * (ROWS // 2))

        @block.scalar
        def _(sc):
            sc.wait_ge(half_ready, 1)
            nc.scalar.activation(table_warm[:], neg_half[:], ACT.Silu)
            for e in range(E1):
                sc.wait_ge(ctx_landed[e], 16)
                nc.scalar.activation(ctx_hi[:, e * KB:(e + 1) * KB, :].rearrange("p k f -> p (k f)"),
                                     stage[:, e * CTX:(e + 1) * CTX], ACT.Copy).then_inc(ctx_hi_ready, 1)

            def hi_x(r):
                sc.wait_ge(xT_ready, r + 1)
                nc.scalar.activation(xT_hi[:], p_xT[:], ACT.Copy).then_inc(xhi_ready, 1)

            def hi_act(r, cols):
                sc.wait_ge(aT_ready, r + 1)
                nc.scalar.activation(aT_hi[:, 0:cols], p_aT[:, 0:cols], ACT.Copy).then_inc(ahi_ready, 1)

            def l1_silu(k, h=p_h):
                sc.wait_ge(h_ready, k + 1)
                nc.scalar.activation(silu[:], h[:], ACT.Silu).then_inc(silu_ready, 1)

            def l2_silus(t):
                sc.wait_ge(z_ready, t + 1)
                nc.scalar.activation(z_silu[:], z[:], ACT.Silu).then_inc(z_silu_ready, 1)
                sc.wait_ge(part_b_ready, t + 1)
                nc.scalar.activation(silu[:, GATED_B:HID], p_b[:, 0:HID - GATED_B], ACT.Silu).then_inc(silu_b_ready, 1)
                sc.wait_ge(part_c_ready, t + 1)
                nc.scalar.activation(silu[:, 0:GATED_B], p_h[:, 0:GATED_B], ACT.Silu).then_inc(silu_ready, 1)

            def split_hi(n):
                piece = bass.ds(n * PIECE, PIECE)
                nc.scalar.activation(w2_hi[:, piece], stage[:, piece], ACT.Copy).then_inc(w2_hi_ready, 1)

            hi_x(0)
            hi_x(1)
            l1_silu(0, p_a)
            for k in range(1, SPLIT0):
                hi_act(k - 1, D)
                l1_silu(k)
                hi_x(k + 1)
            sc.wait_ge(up_landed, 16)
            with sc.Fori(SPLIT0, SPLIT0 + UP_PIECES) as k:
                hi_act(k - 1, D)
                split_hi(k - SPLIT0)
                l1_silu(k)
                hi_x(k + 1)
            sc.wait_ge(down_landed, 16)
            with sc.Fori(SPLIT0 + UP_PIECES, SPLIT0 + PIECES) as k:
                hi_act(k - 1, D)
                split_hi(k - SPLIT0)
                l1_silu(k)
                hi_x(k + 1)
            with sc.Fori(SPLIT0 + PIECES, STEPS) as k:
                hi_act(k - 1, D)
                l1_silu(k)
                hi_x(k + 1)
            hi_act(STEPS - 1, D)
            l2_silus(0)
            hi_x(STEPS + 1)
            with sc.Fori(1, TILES - 1) as t:
                hi_act(STEPS + t - 1, DN)
                l2_silus(t)
                hi_x(STEPS + t + 1)
            hi_act(ROWS - 2, DN)
            l2_silus(TILES - 1)
            hi_act(ROWS - 1, DN)

        @block.vector
        def _(dve):
            done = {sort_step: 0}

            def step(ins):
                done[sort_step] += 1
                ins.then_inc(sort_step, 1)
                dve.wait_ge(sort_step, done[sort_step])

            nc.vector.memset(ones[:], 1.0).then_inc(masks_ready, 1)
            nc.vector.memset(from_e[:, 0, :], 1.0)
            nc.vector.memset(from_e[:, E1, :], 0.0)
            nc.vector.memset(carry[:], 1.0)
            dve.wait_ge(iotas_ready, 4)
            nc.vector.tensor_tensor(below[:], col[:], part[:].broadcast_to([P, P]), ALU.is_gt).then_inc(masks_ready, 1)
            nc.vector.tensor_copy(token_f[:], token[:])
            step(nc.vector.tensor_tensor(ident[:], col[:], part[:].broadcast_to([P, P]), ALU.is_equal))
            nc.vector.memset(carry[:, :, 0:1], 0.0)
            dve.wait_ge(ids_landed, 16)
            for e in range(1, E1):
                last = nc.vector.tensor_scalar(from_e[:, e, :], ids[:], float(VOCAB // E1 * e), None, ALU.is_ge)
            step(last)
            step(nc.vector.tensor_tensor(is_e[:], from_e[:, 0:E1, :], from_e[:, 1:E1 + 1, :], ALU.subtract))
            flat = "p e c -> p (e c)"
            step(nc.vector.tensor_tensor_scan(upto[:].rearrange(flat), carry[:].rearrange(flat),
                                              is_e[:].rearrange(flat), 0.0, ALU.mult, ALU.add))
            nc.vector.tensor_copy(counts[:], upto[:, :, TILES - 1]).then_inc(counts_ready, 1)
            nc.vector.tensor_tensor(before[:], upto[:], is_e[:], ALU.subtract)
            dve.wait_ge(offsets_ready, 1)
            nc.vector.tensor_copy(totals[:, 0, :], p_sort[:, E1:2 * E1])
            step(nc.vector.tensor_scalar(tiles_i[:], p_sort[:, E1:2 * E1], float(P - 1), None, ALU.add))
            step(nc.vector.tensor_scalar(tiles_i[:], tiles_i[:], P.bit_length() - 1, None, ALU.logical_shift_right))
            step(nc.vector.tensor_copy(totals[:, 1, :], tiles_i[:]))
            nc.vector.memset(tot_before[:, :, 0], 0.0)
            step(nc.vector.tensor_copy(tot_before[:, :, 1], totals[:, :, 0]))
            for e in range(2, E1):
                step(nc.vector.tensor_tensor(tot_before[:, :, e], tot_before[:, :, e - 1], totals[:, :, e - 1], ALU.add))
            nc.vector.tensor_tensor(first[:, 0, :], p_sort[:, 0:E1], tot_before[:, 0, :], ALU.add)
            step(nc.vector.scalar_tensor_tensor(first[:, 1, :], tot_before[:, 1, :], float(P), p_sort[:, 0:E1],
                                                ALU.mult, ALU.add))
            every = [P, 2, E1, TILES]
            step(nc.vector.tensor_tensor(slot_e[:], before[:].unsqueeze(1).broadcast_to(every),
                                         first[:].unsqueeze(3).broadcast_to(every), ALU.add))
            step(nc.vector.tensor_tensor(slot_e[:], slot_e[:], is_e[:].unsqueeze(1).broadcast_to(every), ALU.mult))
            step(nc.vector.tensor_reduce(slot_f[:], slot_e[:].rearrange("p m e c -> p m c e"), AX_X, ALU.add))
            step(nc.vector.tensor_copy(slot[:], slot_f[:]))
            nc.vector.tensor_scalar(slot_lo[:], slot[:], P - 1, None, ALU.bitwise_and)
            step(nc.vector.tensor_scalar(slot_hi[:], slot[:], P.bit_length() - 1, None, ALU.logical_shift_right))
            to_steps, to_tiles = [P, TILES, STEPS], [P, TILES, TILES]
            nc.vector.tensor_tensor(put_padded[:, :, 2], col[:, 0:STEPS].unsqueeze(1).broadcast_to(to_steps),
                                    slot_hi[:, 1].unsqueeze(2).broadcast_to(to_steps),
                                    ALU.is_equal).then_inc(owners_ready, 1)

            def one_hot(m, c0, c1):
                some = [P, c1 - c0, P]
                nc.vector.tensor_tensor(in_lo[m][:, c0:c1], col[:].unsqueeze(1).broadcast_to(some),
                                        slot_lo[:, m, c0:c1].unsqueeze(2).broadcast_to(some),
                                        ALU.is_equal).then_inc(onehots_ready, 1)

            def split_ctx(e, half):
                dve.wait_ge(ctx_hi_ready, e + 1)
                blocks = slice(e * KB + half * KB // 2, e * KB + (half + 1) * KB // 2)
                start = e * CTX + half * HALF
                nc.vector.tensor_tensor(ctx_lo[:, blocks, :].rearrange("p k f -> p (k f)"), stage[:, start:start + HALF],
                                        ctx_hi[:, blocks, :].rearrange("p k f -> p (k f)").bitcast(F32),
                                        ALU.subtract).then_inc(ctx_lo_ready, 1)

            one_hot(1, 0, TILES // 2)
            one_hot(1, TILES // 2, TILES)
            step(nc.vector.tensor_scalar(step_ge[:, 0, :], col[0:1, 0:STEPS], tot_before[0:1, 1, 1:2], None, ALU.is_ge))
            step(nc.vector.scalar_tensor_tensor(step_ge[:, 1, :], col[0:1, 0:STEPS], tot_before[0:1, 1, 2:3],
                                                step_ge[:, 0, :], ALU.is_ge, ALU.add))
            nc.vector.scalar_tensor_tensor(step_expert[:], col[0:1, 0:STEPS], tot_before[0:1, 1, 3:4],
                                           step_ge[:, 1, :], ALU.is_ge, ALU.add).then_inc(rows_ready, 1)
            dve.wait_ge(slots_ready, 1)
            nc.vector.tensor_copy(gather_row[:], p_sort[:, 0:STEPS]).then_inc(rows_ready, 1)
            step(nc.vector.tensor_scalar(empty[:], p_sort[:, 2 * STEPS:3 * STEPS], -1.0, 1.0, ALU.mult, ALU.add))
            step(nc.vector.tensor_tensor(empty_row[:], empty[:], pad_row[:], ALU.mult))
            nc.vector.tensor_tensor(x1_row[:], p_sort[:, STEPS:2 * STEPS], empty_row[:], ALU.add).then_inc(rows_ready, 1)
            split_ctx(0, 0)
            split_ctx(0, 1)

            def statistics(row, tile=None, between=None):
                r, half, parity = row
                if tile is None:
                    dve.wait_ge(x_landed[parity], 16 * (half + 1))
                else:
                    dve.wait_ge(x1_landed[tile[2]], 16 * (tile[1] + 1))
                nc.vector.bn_stats(bn6[:, parity, :], x_rows_of(r)).then_inc(bn6_ready, 1)
                dve.wait_ge(bn6_ready, r + 1)
                if between is not None:
                    normalise(between)
                nc.vector.bn_aggr(mean_var[:, parity, :], bn6[:, parity, :]).then_inc(mean_ready, 1)
                dve.wait_ge(mean_ready, r + 1)
                nc.vector.tensor_scalar(var_eps[:, parity:parity + 1], mean_var[:, parity, 1:2], EPS, None,
                                        ALU.add).then_inc(var_ready, 1)

            def normalise(row, first_use=False):
                r, _, parity = row
                dve.wait_ge(rstd_ready, r + 1)
                if not first_use:
                    dve.wait_ge(xT_ready, r - 1)
                nc.vector.tensor_scalar(xn[:, parity, :], x_rows_of(r), mean_var[:, parity, 0:1],
                                        rstd[:, parity:parity + 1], ALU.subtract, ALU.mult).then_inc(xn_ready, 1)

            def lo_x(r):
                dve.wait_ge(xhi_ready, r + 1)
                nc.vector.tensor_tensor(xT_lo[:], p_xT[:], xT_hi[:].bitcast(F32), ALU.subtract).then_inc(xlo_ready, 1)

            def lo_act(r, cols):
                dve.wait_ge(ahi_ready, r + 1)
                nc.vector.tensor_tensor(aT_lo[:, 0:cols], p_aT[:, 0:cols], aT_hi[:, 0:cols].bitcast(F32),
                                        ALU.subtract).then_inc(alo_ready, 1)

            def residual(row, first_use=False, y=p_y):
                r, half, parity = row
                dve.wait_ge(y_ready, r + 1)
                if not first_use:
                    dve.wait_ge(stored[parity], 16 * half)
                nc.vector.tensor_tensor(xout[:, parity, :], y[:], x_rows_of(r), ALU.add).then_inc(xout_ready, 1)

            def l1_gate(k, h=p_h):
                dve.wait_ge(silu_ready, k + 1)
                nc.vector.tensor_tensor(act[:, 0:D], silu[:], h[:], ALU.mult).then_inc(act_ready, 1)

            def l2_gates(t):
                of = 12 * t
                dve.wait_ge(part_a_ready, t + 1)
                nc.vector.tensor_copy(logits[:], p_a[:, ROUTE0:ROUTE0 + E2]).then_inc(router_step, 1)
                dve.wait_ge(router_step, of + 1)
                nc.vector.tensor_reduce(top1[:], logits[:], AX_X, ALU.max).then_inc(router_step, 1)
                nc.vector.max(top8[:], logits[:]).then_inc(router_step, 1)
                dve.wait_ge(router_step, of + 3)
                nc.vector.tensor_scalar(z[:], logits[:], top1[:, 0:1], -1.0, ALU.subtract, ALU.add).then_inc(z_ready, 1)
                nc.vector.max_index(top8_at[:], top8[:], logits[:]).then_inc(router_step, 1)
                dve.wait_ge(router_step, of + 4)
                nc.vector.tensor_scalar(chosen1[:], col[:, 0:E2], top8_at[:, 0:1], None,
                                        ALU.is_equal).then_inc(router_step, 1)
                dve.wait_ge(router_step, of + 5)
                nc.vector.scalar_tensor_tensor(chosen[:], col[:, 0:E2], top8_at[:, 1:2], chosen1[:],
                                               ALU.is_equal, ALU.add).then_inc(router_step, 1)
                dve.wait_ge(z_silu_ready, t + 1)
                nc.vector.tensor_tensor(z_rest[:], z[:], z_silu[:], ALU.subtract).then_inc(router_step, 1)
                dve.wait_ge(router_step, of + 7)
                nc.vector.reciprocal(z_rest_inv[:], z_rest[:]).then_inc(router_step, 1)
                dve.wait_ge(router_step, of + 8)
                nc.vector.tensor_tensor(z_exp[:], z_silu[:], z_rest_inv[:], ALU.mult).then_inc(router_step, 1)
                dve.wait_ge(router_step, of + 9)
                nc.vector.tensor_reduce(z_sum[:], z_exp[:], AX_X, ALU.add).then_inc(router_step, 1)
                dve.wait_ge(router_step, of + 10)
                nc.vector.reciprocal(z_sum_inv[:], z_sum[:]).then_inc(router_step, 1)
                dve.wait_ge(router_step, of + 11)
                nc.vector.scalar_tensor_tensor(gates[:], z_exp[:], z_sum_inv[:, 0:1], chosen[:],
                                               ALU.mult, ALU.mult).then_inc(router_step, 1)
                dve.wait_ge(router_step, of + 12)

            def l2_act(r, t):
                by_expert = "p (e f) -> p e f"
                half = E2 // 2
                nc.vector.tensor_tensor(act[:, HID:DN].rearrange(by_expert, e=E2),
                                        p_a[:, 0:LORA].rearrange(by_expert, e=E2),
                                        gates[:].unsqueeze(2).broadcast_to([P, E2, LR]), ALU.mult)
                nc.vector.tensor_tensor(up_gated[:, 0:HID // 2].rearrange(by_expert, e=half),
                                        p_a[:, UP_A0:GATE_B0].rearrange(by_expert, e=half),
                                        gates[:, 0:half].unsqueeze(2).broadcast_to([P, half, FE]), ALU.mult)
                dve.wait_ge(silu_b_ready, t + 1)
                nc.vector.tensor_tensor(up_gated[:, HID // 2:HID].rearrange(by_expert, e=half),
                                        p_b[:, UP_B0 - GATE_B0:GATE_C0 - GATE_B0].rearrange(by_expert, e=half),
                                        gates[:, half:E2].unsqueeze(2).broadcast_to([P, half, FE]),
                                        ALU.mult).then_inc(up_gated_ready, 1)
                dve.wait_ge(up_gated_ready, t + 1)
                dve.wait_ge(silu_ready, r + 1)
                nc.vector.tensor_tensor(act[:, 0:HID], silu[:], up_gated[:], ALU.mult).then_inc(act_ready, 1)

            for r in range(2):
                statistics(one(r))
            normalise(one(0), first_use=True)
            split_ctx(1, 0)
            lo_x(0)
            normalise(one(1), first_use=True)
            statistics(one(2))
            split_ctx(1, 1)
            split_ctx(2, 0)
            split_ctx(2, 1)
            dve.wait_ge(h_ready, 1)
            lo_x(1)
            l1_gate(0, p_a)
            statistics(one(3), between=one(2))
            lo_act(0, D)
            split_ctx(3, 0)
            statistics(one(4), between=one(3))
            l1_gate(1)
            lo_x(2)
            split_ctx(3, 1)
            step(nc.vector.tensor_tensor(in_tile[:], col[:, 0:TILES].unsqueeze(1).broadcast_to(to_tiles),
                                         slot_hi[:, 0].unsqueeze(2).broadcast_to(to_tiles), ALU.is_equal))
            nc.vector.tensor_tensor(put_compact[:], in_tile[:], token_f[:].unsqueeze(2).broadcast_to(to_tiles), ALU.mult)
            one_hot(0, 0, TILES)
            for k in range(2, 4):
                lo_act(k - 1, D)
                if k == 2:
                    dve.wait_ge(slots_ready, 2)
                    nc.vector.tensor_copy(out_row[:], p_sort[:, COMPACT0:COMPACT0 + TILES]).then_inc(rows_ready, 1)
                residual(one(k - 2), first_use=True)
                statistics(one(k + 3), between=one(k + 2))
                l1_gate(k)
                lo_x(k + 1)
            with dve.Fori(2, (STEPS - 3) // 2) as h:
                for u in range(2):
                    k = 2 * h + u
                    lo_act(k - 1, D)
                    residual(pair(h, u - 2))
                    statistics(pair(h, u + 3), between=pair(h, u + 2))
                    l1_gate(k)
                    lo_x(k + 1)
            for k in range(STEPS - 3, STEPS):
                lo_act(k - 1, D)
                residual(one(k - 2))
                statistics(one(k + 3), tile=one(k + 3 - STEPS), between=one(k + 2))
                l1_gate(k)
                lo_x(k + 1)

            r = STEPS
            lo_act(r - 1, D)
            residual(one(r - 2))
            statistics(one(r + 3), tile=one(3), between=one(r + 2))
            l2_gates(0)
            l2_act(r, 0)
            lo_x(r + 1)
            with dve.Fori(0, (TILES - 4) // 2) as h:
                for u in range(2):
                    t = 2 * h + u + 1
                    c = STEPS + 1 + u
                    lo_act(2 * h + c - 1, DN)
                    residual(pair(h, c - 2))
                    statistics(pair(h, c + 3), tile=pair(h, u + 4), between=pair(h, c + 2))
                    l2_gates(t)
                    l2_act(2 * h + c, t)
                    lo_x(2 * h + c + 1)
            for t in range(TILES - 3, TILES):
                r = STEPS + t
                lo_act(r - 1, DN)
                residual(one(r - 2))
                if r + 2 < ROWS:
                    normalise(one(r + 2))
                l2_gates(t)
                l2_act(r, t)
                if r + 1 < ROWS:
                    lo_x(r + 1)
            dve.wait_ge(y_ready, ROWS - 1)
            lo_act(ROWS - 1, DN)
            residual(one(ROWS - 2))
            residual(one(ROWS - 1), y=p_h)

        @block.tensor
        def _(pe):
            pe.wait_ge(masks_ready, 2)
            pe.wait_ge(counts_ready, 1)
            nc.tensor.matmul(p_sort[:, 0:E1], below[:], counts[:], start=True, stop=True)
            nc.tensor.matmul(p_sort[:, E1:2 * E1], ones[:], counts[:], start=True, stop=True).then_inc(offsets_ready, 1)
            pe.wait_ge(puts_ready, 2)
            for c in range(TILES):
                if c % (TILES // 2) == 0:
                    pe.wait_ge(onehots_ready, c // (TILES // 2) + 1)
                last = nc.tensor.matmul(p_sort[:, 0:3 * STEPS], in_lo[1][:, c, :],
                                        put_padded[:, c].rearrange("p v s -> p (v s)"),
                                        start=(c == 0), stop=(c == TILES - 1))
            last.then_inc(slots_ready, 1)

            def compact_slots():
                pe.wait_ge(onehots_ready, 3)
                for c in range(TILES):
                    last = nc.tensor.matmul(p_sort[:, COMPACT0:COMPACT0 + TILES], in_lo[0][:, c, :], put_compact[:, c, :],
                                            start=(c == 0), stop=(c == TILES - 1))
                last.then_inc(slots_ready, 1)

            def blk(i):
                return slice(i * P, (i + 1) * P)

            def turn_x(r, parity):
                pe.wait_ge(xn_ready, r + 1)
                for i in range(KB):
                    last = nc.tensor.transpose(p_xT[:, blk(i)], xn[:, parity, blk(i)], ident[:])
                last.then_inc(xT_ready, 1)

            def turn_act(r, blocks):
                pe.wait_ge(act_ready, r + 1)
                for i in range(blocks):
                    last = nc.tensor.transpose(p_aT[:, blk(i)], act[:, blk(i)], ident[:])
                last.then_inc(aT_ready, 1)

            def hi_passes(to, hi, blocks, w_hi, w_lo):
                for i in range(blocks):
                    nc.tensor.matmul(to, hi[:, blk(i)], w_hi(i), start=(i == 0), stop=False)
                    nc.tensor.matmul(to, hi[:, blk(i)], w_lo(i), start=False, stop=False)

            def lo_passes(to, lo, blocks, w_hi):
                for i in range(blocks):
                    last = nc.tensor.matmul(to, lo[:, blk(i)], w_hi(i), start=False, stop=(i == blocks - 1))
                return last

            def l1_matrix(k):
                e = pe.value_load(step_expert[0:1, bass.ds(k, 1)], min_val=0, max_val=E1 - 1)
                return e, [lambda i, w=w: w[:, bass.ds(e * KB + i, 1), :].rearrange("p a f -> p (a f)")
                           for w in (ctx_hi, ctx_lo)]

            def l1_first(k, to=p_h, between=None, some_split=False):
                e, w = l1_matrix(k)
                if some_split:
                    pe.wait_ge(ctx_lo_ready, 2 * e + 2)
                pe.wait_ge(xhi_ready, k + 1)
                hi_passes(to[:], xT_hi, KB, *w)
                if between is not None:
                    between()
                pe.wait_ge(xlo_ready, k + 1)
                lo_passes(to[:], xT_lo, KB, w[0]).then_inc(h_ready, 1)

            def l1_second(k, first_use=False):
                e, w = l1_matrix(k)
                if not first_use:
                    pe.wait_ge(xout_ready, k)
                pe.wait_ge(ahi_ready, k + 1)
                hi_passes(p_y[:], aT_hi, KB, *w)
                pe.wait_ge(alo_ready, k + 1)
                lo_passes(p_y[:], aT_lo, KB, w[0]).then_inc(y_ready, 1)

            def up_part(c0, c1):
                return [lambda i, w=w: w[:, i * UPW + c0:i * UPW + c1] for w in (w2_hi, w2_lo)]

            down = [lambda i, w=w: w[:, DOWN0 + i * D:DOWN0 + (i + 1) * D] for w in (w2_hi, w2_lo)]

            def l2_first(r):
                pe.wait_ge(xhi_ready, r + 1)
                for to, c0, c1, ready in ((p_a, 0, GATE_B0, part_a_ready), (p_b, GATE_B0, GATE_C0, part_b_ready),
                                          (p_h, GATE_C0, UPW, part_c_ready)):
                    w = up_part(c0, c1)
                    hi_passes(to[:, 0:c1 - c0], xT_hi, KB, *w)
                    pe.wait_ge(xlo_ready, r + 1)
                    lo_passes(to[:, 0:c1 - c0], xT_lo, KB, w[0]).then_inc(ready, 1)

            def l2_second(r, to=p_y, between=None):
                if to is p_y:
                    pe.wait_ge(xout_ready, r)
                pe.wait_ge(ahi_ready, r + 1)
                hi_passes(to[:], aT_hi, DB, *down)
                pe.wait_ge(alo_ready, r + 1)
                if between is not None:
                    between()
                lo_passes(to[:], aT_lo, DB, down[0]).then_inc(y_ready, 1)

            pe.wait_ge(rows_ready, 1)

            def turn_x1():
                pe.wait_ge(xlo_ready, 1)
                turn_x(1, 1)

            turn_x(0, 0)
            l1_first(0, to=p_a, between=turn_x1, some_split=True)
            l1_first(1, between=lambda: turn_act(0, KB), some_split=True)
            turn_x(2, 0)
            l1_second(0, first_use=True)
            compact_slots()
            pe.wait_ge(ctx_lo_ready, 2 * E1)
            turn_act(1, KB)
            l1_first(2)
            turn_x(3, 1)
            l1_second(1)
            with pe.Fori(1, (STEPS - 1) // 2) as h:
                for u in range(1, 3):
                    k = 2 * h + u
                    turn_act(k - 1, KB)
                    l1_first(k)
                    turn_x(k + 1, (u + 1) % 2)
                    l1_second(k - 1)
            pe.wait_ge(w2_lo_ready, PIECES)
            turn_act(STEPS - 1, KB)
            l2_first(STEPS)
            turn_x(STEPS + 1, (STEPS + 1) % 2)
            l1_second(STEPS - 1)
            with pe.Fori(0, (TILES - 2) // 2) as h:
                for u in range(2):
                    r = 2 * h + STEPS + 1 + u
                    turn_act(r - 1, DB)
                    l2_first(r)
                    turn_x(r + 1, (STEPS + 2 + u) % 2)
                    l2_second(r - 1)
            turn_act(ROWS - 2, DB)
            l2_first(ROWS - 1)
            l2_second(ROWS - 2, between=lambda: turn_act(ROWS - 1, DB))
            l2_second(ROWS - 1, to=p_h)


def kernel(x, itok_BxS_13_99985, ctx_2048, L0_ffn_G, L0_ffn_gate_w, L0_ffn_up_w, L0_ffn_down_w, L0_ffn_lora_A,
           L0_ffn_lora_B):
    import numpy as np
    import concourse.bacc as bacc
    from concourse.bass_utils import run_bass_kernel_spmd

    def blocks(m):
        return np.ascontiguousarray(m.reshape(-1, P, m.shape[-1]).transpose(1, 0, 2)).reshape(P, -1)

    ctx = np.asarray(ctx_2048)
    gate, up, lora_a = (np.asarray(a).reshape(-1, D).T for a in (L0_ffn_gate_w, L0_ffn_up_w, L0_ffn_lora_A))
    down, lora_b = (np.asarray(a).transpose(0, 2, 1).reshape(-1, D) for a in (L0_ffn_down_w, L0_ffn_lora_B))
    arrays = {
        "x": np.ascontiguousarray(np.asarray(x).reshape(TOKENS, D)),
        "token_ids": np.ascontiguousarray(np.asarray(itok_BxS_13_99985).reshape(P, TILES)),
        "ctx_t": np.ascontiguousarray(ctx.transpose(0, 2, 1).reshape(E1, KB, P, D).transpose(2, 0, 1, 3)).reshape(P, E1, CTX),
        "w_up": blocks(np.concatenate([lora_a, np.asarray(L0_ffn_G), up[:, :HID // 2], gate[:, GATED_B:],
                                       up[:, HID // 2:], gate[:, :GATED_B]], axis=1)),
        "w_down": blocks(np.concatenate([down, lora_b], axis=0)),
    }
    nc = bacc.Bacc("TRN2", target_bir_lowering=False, num_devices=1)
    args = [nc.dram_tensor(n, a.shape, mybir.dt.from_np(a.dtype), kind="ExternalInput").ap() for n, a in arrays.items()]
    out = nc.dram_tensor("out", [TOKENS, D], F32, kind="ExternalOutput").ap()
    build(nc, *args, out)
    result = run_bass_kernel_spmd(nc, [arrays], core_ids=[0])
    return result.results[0]["out"].reshape(4, 512, D)
```

```python
from contextlib import ExitStack

import concourse.bass as bass
from concourse import mybir

F32 = mybir.dt.float32
F32R = mybir.dt.float32r
F16 = mybir.dt.float16
I32 = mybir.dt.int32
U32 = mybir.dt.uint32
ALU = mybir.AluOpType
ACT = mybir.ActivationFunctionType
AX_X = mybir.AxisListType.X

P = 128
D = 512
KB = D // P
TOKENS = 4 * 512
TILES = TOKENS // P
E1, VOCAB = 4, 25000
STEPS = TILES + E1 - 1
ROWS = STEPS + TILES
E2, FE, LR = 8, 64, 16
HID = E2 * FE
LORA = E2 * LR
ROUTE0 = LORA
UP_A0 = LORA + E2
GATE_B0 = UP_A0 + HID // 2
UP_B0 = GATE_B0 + 2 * FE
GATE_C0 = UP_B0 + HID // 2
GATED_B = HID - 2 * FE
UPW = GATE_C0 + GATED_B
DN = HID + LORA
DB = DN // P
EPS = 1e-5
COMPACT0 = 64
XRING = 8
CTX = KB * D
HALF = CTX // 2
W2 = KB * UPW + DB * D
DOWN0 = KB * UPW
PIECES = 15
PIECE = W2 // PIECES
SPLIT0 = STEPS - PIECES
UP_PIECES = DOWN0 // PIECE
WARM = 16


def build(nc, x, token_ids, ctx_t, w_up, w_down, out):
    x1_rows = nc.dram_tensor("x1_rows", [TOKENS + STEPS * P, D], F32, kind="Internal").ap()

    with ExitStack() as stack:
        def sb(name, shape, dt=F32):
            return stack.enter_context(nc.sbuf_tensor(name, shape, dt))

        def ps(name, cols):
            return stack.enter_context(nc.psum_tensor(name, [P, cols], F32))

        def sem(name):
            return stack.enter_context(nc.semaphore(name))

        stage = sb("stage", [P, E1 * CTX])
        ctx_hi, ctx_lo = (sb(n, [P, E1 * KB, D], F32R) for n in ("ctx_hi", "ctx_lo"))
        w2_hi, w2_lo = (sb(n, [P, W2], F32R) for n in ("w2_hi", "w2_lo"))
        xin = sb("xin", [P, XRING, D])
        xn = sb("xn", [P, 2, D])
        xT_hi, xT_lo = (sb(n, [P, KB * P], F32R) for n in ("xT_hi", "xT_lo"))
        silu = sb("silu", [P, D])
        up_gated = sb("up_gated", [P, HID])
        act = sb("act", [P, DN])
        aT_hi, aT_lo = (sb(n, [P, DB * P], F32R) for n in ("aT_hi", "aT_lo"))
        xout = sb("xout", [P, 2, D])
        bn6 = sb("bn6", [P, 2, 6])
        mean_var = sb("mean_var", [P, 2, 2])
        var_eps = sb("var_eps", [P, 2])
        rstd = sb("rstd", [P, 2])
        neg_half = sb("neg_half", [P, 1])
        logits = sb("logits", [P, E2])
        top1, top8 = sb("top1", [P, 1]), sb("top8", [P, 8])
        top8_at = sb("top8_at", [P, 8], U32)
        chosen1, chosen = sb("chosen1", [P, E2]), sb("chosen", [P, E2])
        z, z_silu, z_rest, z_rest_inv, z_exp, gates = (
            sb(n, [P, E2]) for n in ("z", "z_silu", "z_rest", "z_rest_inv", "z_exp", "gates"))
        z_sum, z_sum_inv = sb("z_sum", [P, 1]), sb("z_sum_inv", [P, 1])
        col = sb("col", [P, P], I32)
        part = sb("part", [P, 1], I32)
        token = sb("token", [P, TILES], I32)
        token_f = sb("token_f", [P, TILES])
        table_warm = sb("table_warm", [P, 1])
        pad_row = sb("pad_row", [P, STEPS], I32)
        ident = sb("ident", [P, P])
        below = sb("below", [P, P])
        ones = sb("ones", [P, P])
        ids = sb("ids", [P, TILES], I32)
        from_e = sb("from_e", [P, E1 + 1, TILES])
        is_e = sb("is_e", [P, E1, TILES])
        carry = sb("carry", [P, E1, TILES])
        upto = sb("upto", [P, E1, TILES])
        upto_own = sb("upto_own", [P, E1, TILES])
        own = sb("own", [P, TILES])
        tile_start = sb("tile_start", [P, TILES])
        tile_used = sb("tile_used", [P, E1, TILES])
        totals = sb("totals", [P, 2, E1])
        counts = sb("counts", [P, E1])
        tot_before = sb("tot_before", [P, 2, E1])
        first = sb("first", [P, 2, E1])
        first_e = sb("first_e", [P, 2, E1, TILES])
        first_own = sb("first_own", [P, 2, TILES])
        slot_f = sb("slot_f", [P, TILES])
        slot = sb("slot", [P, 2, TILES], I32)
        slot_lo, slot_hi = sb("slot_lo", [P, 2, TILES], I32), sb("slot_hi", [P, 2, TILES], I32)
        def as_one_hot(m):
            return m.bitcast(F16).rearrange("p (c q) -> p c q", q=P)
        in_lo_padded = [as_one_hot(b[:].rearrange("p a d -> p (a d)")[:, 0:TILES // 2 * P // 2]) for b in (xout, xn)]
        in_lo_compact = [as_one_hot(up_gated[:]), as_one_hot(stage[:, E1 * CTX - TILES // 2 * P // 2:E1 * CTX])]
        in_tile = sb("in_tile", [P, TILES, TILES], F16)
        put_padded = sb("put_padded", [P, TILES, 3, STEPS], F16)
        put_compact = sb("put_compact", [P, TILES, TILES], F16)
        empty = sb("empty", [P, STEPS])
        empty_row = sb("empty_row", [P, STEPS])
        gather_row = sb("gather_row", [P, STEPS], U32)
        x1_row = sb("x1_row", [P, STEPS], U32)
        out_row = sb("out_row", [P, TILES], U32)
        step_ge = sb("step_ge", [1, 2, STEPS])
        step_expert = sb("step_expert", [1, STEPS], I32)

        p_xT, p_h, p_a, p_b, p_y = (ps(n, 512) for n in ("p_xT", "p_h", "p_a", "p_b", "p_y"))
        p_aT = ps("p_aT", 1024)
        p_sort = ps("p_sort", 512)

        ids_landed, up_landed, down_landed = sem("ids_landed"), sem("up_landed"), sem("down_landed")
        ctx_landed = [sem(f"ctx_landed{e}") for e in range(E1)]
        iotas_ready, sort_step, masks_ready = sem("iotas_ready"), sem("sort_step"), sem("masks_ready")
        counts_ready, offsets_ready = sem("counts_ready"), sem("offsets_ready")
        owners_ready, puts_ready, onehots_ready = sem("owners_ready"), sem("puts_ready"), sem("onehots_ready")
        slots_ready, rows_ready = sem("slots_ready"), sem("rows_ready")
        half_ready = sem("half_ready")
        ctx_hi_ready = sem("ctx_hi_ready")
        ctx_lo_half_ready = sem("ctx_lo_half_ready")
        ctx_lo_ready = sem("ctx_lo_ready")
        w2_hi_ready, w2_lo_ready = sem("w2_hi_ready"), sem("w2_lo_ready")
        x_landed = [sem("x_landed0"), sem("x_landed1")]
        x1_landed = [sem("x1_landed0"), sem("x1_landed1")]
        bn6_ready, mean_ready, var_ready = sem("bn6_ready"), sem("mean_ready"), sem("var_ready")
        rstd_ready, xn_ready, xT_ready = sem("rstd_ready"), sem("xn_ready"), sem("xT_ready")
        xhi_ready, xlo_ready = sem("xhi_ready"), sem("xlo_ready")
        silu_ready, act_ready, aT_ready = sem("silu_ready"), sem("act_ready"), sem("aT_ready")
        ahi_ready, alo_ready = sem("ahi_ready"), sem("alo_ready")
        y_ready, xout_ready = sem("y_ready"), sem("xout_ready")
        stored = [sem("stored0"), sem("stored1")]
        h_ready = sem("h_ready")
        part_a_ready, part_b_ready, part_c_ready = sem("part_a_ready"), sem("part_b_ready"), sem("part_c_ready")
        silu_b_ready, up_gated_ready = sem("silu_b_ready"), sem("up_gated_ready")
        z_ready, z_silu_ready = sem("z_ready"), sem("z_silu_ready")
        router_step = sem("router_step")

        block = stack.enter_context(nc.Block())

        def pair(h, c):
            return 2 * h + c, h + c // 2, c % 2

        def one(r):
            return r, r // 2, r % 2

        def x_rows_of(r):
            return xin[:, bass.ds(r % XRING, 1), :].rearrange("p a d -> p (a d)")

        def ctx_half(e, half):
            blocks = slice(e * KB + half * KB // 2, e * KB + (half + 1) * KB // 2)
            start = e * CTX + half * HALF
            return (ctx_lo[:, blocks, :].rearrange("p k f -> p (k f)"), stage[:, start:start + HALF],
                    ctx_hi[:, blocks, :].rearrange("p k f -> p (k f)"))

        @block.sync
        def _(sp):
            sp.dma_start(ids[:], token_ids).then_inc(ids_landed, 16)
            for e in range(E1):
                if e == E1 - 1:
                    sp.wait_ge(x_landed[0], 16)
                sp.dma_start(stage[:, e * CTX:(e + 1) * CTX], ctx_t[:, e, :]).then_inc(ctx_landed[e], 16)
            sp.wait_ge(ctx_lo_half_ready, 1)
            sp.wait_ge(ctx_lo_ready, 2 * (DOWN0 // CTX) + 1)
            for i in range(KB):
                r = i + 5
                sp.wait_ge(x_landed[r % 2], 16 * (r // 2 + 1))
                sp.dma_start(stage[:, i * UPW:(i + 1) * UPW], w_up[:, i * UPW:(i + 1) * UPW]).then_inc(up_landed, 16)
            sp.wait_ge(ctx_lo_ready, 2 * E1 - 1)
            sp.dma_start(stage[:, DOWN0:W2], w_down).then_inc(down_landed, 16)
            for t in range(TILES):
                r = STEPS + t
                sp.wait_ge(stored[0], 16 * ((t + 3) // 2 + 1))
                sp.wait_ge(stored[1], 16 * ((t + 4) // 2))
                sp.wait_ge(xout_ready, r - XRING + 1)
                if t >= 2:
                    sp.wait_ge(x1_landed[t % 2], 16 * (t // 2))
                sp.dma_start(xin[:, r % XRING, :], x1_rows[t * P:(t + 1) * P, :]).then_inc(x1_landed[t % 2], 16)

        @block.gpsimd
        def _(pool):
            nc.gpsimd.memset(neg_half[:], -0.5).then_inc(half_ready, 1)
            nc.gpsimd.iota(col[:], [[1, P]], base=0, channel_multiplier=0).then_inc(iotas_ready, 1)
            nc.gpsimd.iota(part[:], [[1, 1]], base=0, channel_multiplier=1).then_inc(iotas_ready, 1)
            nc.gpsimd.iota(token[:], [[1, TILES]], base=0, channel_multiplier=TILES).then_inc(iotas_ready, 1)
            nc.gpsimd.iota(pad_row[:], [[P, STEPS]], base=TOKENS, channel_multiplier=1).then_inc(iotas_ready, 1)
            pool.wait_ge(half_ready, 1)

            def gather(r):
                if r >= XRING:
                    pool.wait_ge(xout_ready, r - XRING + 1)
                if r >= 2:
                    pool.wait_ge(x_landed[r % 2], 16 * (r // 2))
                nc.gpsimd.indirect_dma_start(
                    out=xin[:, r % XRING, :], out_offset=None, in_=x,
                    in_offset=bass.IndirectOffsetOnAxis(ap=gather_row[:, r:r + 1], axis=0),
                ).then_inc(x_landed[r % 2], 16)

            def inverse_deviation(r):
                pool.wait_ge(var_ready, r + 1)
                nc.gpsimd.tensor_tensor(rstd[:, r % 2:r % 2 + 1], var_eps[:, r % 2:r % 2 + 1], neg_half[:],
                                        ALU.pow).then_inc(rstd_ready, 1)

            def store(r):
                pool.wait_ge(xout_ready, r + 1)
                to, rows = (x1_rows, x1_row[:, r:r + 1]) if r < STEPS else (out, out_row[:, r - STEPS:r - STEPS + 1])
                nc.gpsimd.indirect_dma_start(
                    out=to, out_offset=bass.IndirectOffsetOnAxis(ap=rows, axis=0), in_=xout[:, r % 2, :],
                    in_offset=None).then_inc(stored[r % 2], 16)

            def split_ctx(e, half, ready):
                pool.wait_ge(ctx_hi_ready, e + 1)
                lo, whole, hi = ctx_half(e, half)
                nc.gpsimd.tensor_tensor(lo, whole, hi.bitcast(F32), ALU.subtract).then_inc(ready, 1)

            def split_lo(n):
                pool.wait_ge(w2_hi_ready, n + 1)
                piece = slice(n * PIECE, (n + 1) * PIECE)
                nc.gpsimd.tensor_tensor(w2_lo[:, piece], stage[:, piece], w2_hi[:, piece].bitcast(F32),
                                        ALU.subtract).then_inc(w2_lo_ready, 1)

            to_steps = [P, TILES, STEPS]
            pool.wait_ge(owners_ready, 1)
            nc.gpsimd.tensor_tensor(put_padded[:, :, 0], put_padded[:, :, 2],
                                    token_f[:].unsqueeze(2).broadcast_to(to_steps), ALU.mult).then_inc(puts_ready, 1)
            pool.wait_ge(owners_ready, 2)
            nc.gpsimd.tensor_tensor(put_padded[:, :, 1], put_padded[:, :, 2],
                                    slot_f[:].unsqueeze(2).broadcast_to(to_steps), ALU.mult).then_inc(puts_ready, 1)
            pool.wait_ge(rows_ready, 2)
            gather(0)
            gather(1)
            split_ctx(0, 1, ctx_lo_half_ready)
            for r in range(2):
                inverse_deviation(r)
                gather(r + 2)
            inverse_deviation(2)
            pool.wait_ge(ctx_lo_ready, 2 * E1 - 3)
            for half in range(2):
                gather(half + 4)
                split_ctx(E1 - 1, half, ctx_lo_ready)
            pool.wait_ge(rows_ready, 3)
            for k in range(ROWS + 2):
                if k - 2 == STEPS:
                    pool.wait_ge(rows_ready, 4)
                if k >= 2:
                    store(k - 2)
                if k + 3 < ROWS:
                    inverse_deviation(k + 3)
                if k + 6 < STEPS:
                    gather(k + 6)
                if SPLIT0 <= k < SPLIT0 + PIECES:
                    split_lo(k - SPLIT0)
            pool.wait_ge(stored[0], 16 * ((ROWS + 1) // 2))
            pool.wait_ge(stored[1], 16 * (ROWS // 2))

        @block.scalar
        def _(sc):
            sc.wait_ge(half_ready, 1)
            nc.scalar.activation(table_warm[:], neg_half[:], ACT.Silu)

            def split_ctx_hi(e):
                sc.wait_ge(ctx_landed[e], 16)
                nc.scalar.activation(ctx_hi[:, e * KB:(e + 1) * KB, :].rearrange("p k f -> p (k f)"),
                                     stage[:, e * CTX:(e + 1) * CTX], ACT.Copy).then_inc(ctx_hi_ready, 1)

            def hi_x(r):
                sc.wait_ge(xT_ready, r + 1)
                nc.scalar.activation(xT_hi[:], p_xT[:], ACT.Copy).then_inc(xhi_ready, 1)

            def hi_act(r, cols):
                sc.wait_ge(aT_ready, r + 1)
                nc.scalar.activation(aT_hi[:, 0:cols], p_aT[:, 0:cols], ACT.Copy).then_inc(ahi_ready, 1)

            def l1_silu(k, h=p_h):
                sc.wait_ge(h_ready, k + 1)
                nc.scalar.activation(silu[:], h[:], ACT.Silu).then_inc(silu_ready, 1)

            def l2_silus(t):
                sc.wait_ge(z_ready, t + 1)
                nc.scalar.activation(z_silu[:], z[:], ACT.Silu).then_inc(z_silu_ready, 1)
                sc.wait_ge(part_b_ready, t + 1)
                nc.scalar.activation(silu[:, GATED_B:HID], p_b[:, 0:HID - GATED_B], ACT.Silu).then_inc(silu_b_ready, 1)
                sc.wait_ge(part_c_ready, t + 1)
                nc.scalar.activation(silu[:, 0:GATED_B], p_h[:, 0:GATED_B], ACT.Silu).then_inc(silu_ready, 1)

            def split_hi(n):
                piece = bass.ds(n * PIECE, PIECE)
                nc.scalar.activation(w2_hi[:, piece], stage[:, piece], ACT.Copy).then_inc(w2_hi_ready, 1)

            for e in range(E1 - 1):
                split_ctx_hi(e)
            hi_x(0)
            split_ctx_hi(E1 - 1)
            hi_x(1)
            l1_silu(0, p_a)
            for k in range(1, SPLIT0):
                hi_act(k - 1, D)
                l1_silu(k)
                hi_x(k + 1)
            sc.wait_ge(up_landed, 16 * KB)
            with sc.Fori(SPLIT0, SPLIT0 + UP_PIECES) as k:
                hi_act(k - 1, D)
                split_hi(k - SPLIT0)
                l1_silu(k)
                hi_x(k + 1)
            sc.wait_ge(down_landed, 16)
            with sc.Fori(SPLIT0 + UP_PIECES, SPLIT0 + PIECES) as k:
                hi_act(k - 1, D)
                split_hi(k - SPLIT0)
                l1_silu(k)
                hi_x(k + 1)
            hi_act(STEPS - 1, D)
            l2_silus(0)
            hi_x(STEPS + 1)
            with sc.Fori(1, TILES - 1) as t:
                hi_act(STEPS + t - 1, DN)
                l2_silus(t)
                hi_x(STEPS + t + 1)
            hi_act(ROWS - 2, DN)
            l2_silus(TILES - 1)
            hi_act(ROWS - 1, DN)

        @block.vector
        def _(dve):
            done = {sort_step: 0}

            def step(ins):
                done[sort_step] += 1
                ins.then_inc(sort_step, 1)
                dve.wait_ge(sort_step, done[sort_step])

            nc.vector.memset(ones[:], 1.0).then_inc(masks_ready, 1)
            nc.vector.memset(from_e[:, 0, :], 1.0)
            nc.vector.memset(from_e[:, E1, :], 0.0)
            nc.vector.memset(carry[:], 1.0)
            dve.wait_ge(iotas_ready, 4)
            nc.vector.tensor_tensor(below[:], col[:], part[:].broadcast_to([P, P]), ALU.is_gt).then_inc(masks_ready, 1)
            nc.vector.tensor_copy(token_f[:], token[:])
            nc.vector.tensor_scalar(tile_start[:], col[:, 0:TILES], float(P), None, ALU.mult)
            nc.vector.memset(tot_before[:, :, 0], 0.0)
            step(nc.vector.tensor_tensor(ident[:], col[:], part[:].broadcast_to([P, P]), ALU.is_equal))
            nc.vector.memset(carry[:, :, 0:1], 0.0)
            dve.wait_ge(ids_landed, 16)
            for e in range(1, E1):
                last = nc.vector.tensor_scalar(from_e[:, e, :], ids[:], float(VOCAB // E1 * e), None, ALU.is_ge)
            step(last)
            step(nc.vector.tensor_tensor(is_e[:], from_e[:, 0:E1, :], from_e[:, 1:E1 + 1, :], ALU.subtract))
            flat = "p e c -> p (e c)"
            step(nc.vector.tensor_tensor_scan(upto[:].rearrange(flat), carry[:].rearrange(flat),
                                              is_e[:].rearrange(flat), 0.0, ALU.mult, ALU.add))
            nc.vector.tensor_copy(counts[:], upto[:, :, TILES - 1]).then_inc(counts_ready, 1)
            step(nc.vector.tensor_tensor(upto_own[:], upto[:], is_e[:], ALU.mult))
            nc.vector.tensor_reduce(own[:], upto_own[:].rearrange("p e c -> p c e"), AX_X, ALU.add)
            dve.wait_ge(offsets_ready, 1)
            each = [P, E1, TILES]
            nc.vector.tensor_copy(totals[:, 0, :], p_sort[:, E1:2 * E1])
            step(nc.vector.tensor_tensor(tile_used[:], p_sort[:, E1:2 * E1].unsqueeze(2).broadcast_to(each),
                                         tile_start[:].unsqueeze(1).broadcast_to(each), ALU.is_gt))
            step(nc.vector.tensor_reduce(totals[:, 1, :], tile_used[:], AX_X, ALU.add))
            for m in range(2):
                last = nc.vector.tensor_tensor_scan(tot_before[:, m, 1:E1], ones[:, 1:E1], totals[:, m, 0:E1 - 1], 0.0,
                                                    ALU.mult, ALU.add)
            step(last)
            nc.vector.tensor_tensor(first[:, 0, :], p_sort[:, 0:E1], tot_before[:, 0, :], ALU.add)
            step(nc.vector.scalar_tensor_tensor(first[:, 1, :], tot_before[:, 1, :], float(P), p_sort[:, 0:E1],
                                                ALU.mult, ALU.add))
            every = [P, 2, E1, TILES]
            step(nc.vector.tensor_tensor(first_e[:], is_e[:].unsqueeze(1).broadcast_to(every),
                                         first[:].unsqueeze(3).broadcast_to(every), ALU.mult))
            step(nc.vector.tensor_reduce(first_own[:], first_e[:].rearrange("p m e c -> p m c e"), AX_X, ALU.add))
            step(nc.vector.scalar_tensor_tensor(slot[:], first_own[:], -1.0,
                                                own[:].unsqueeze(1).broadcast_to([P, 2, TILES]), ALU.add, ALU.add))
            nc.vector.tensor_scalar(slot_lo[:], slot[:], P - 1, None, ALU.bitwise_and)
            step(nc.vector.tensor_scalar(slot_hi[:], slot[:], P.bit_length() - 1, None, ALU.logical_shift_right))
            to_steps, to_tiles = [P, TILES, STEPS], [P, TILES, TILES]
            nc.vector.tensor_tensor(put_padded[:, :, 2], col[:, 0:STEPS].unsqueeze(1).broadcast_to(to_steps),
                                    slot_hi[:, 1].unsqueeze(2).broadcast_to(to_steps),
                                    ALU.is_equal).then_inc(owners_ready, 1)
            nc.vector.tensor_copy(slot_f[:], slot[:, 0]).then_inc(owners_ready, 1)

            def one_hot(to, m, half):
                shape = [P, TILES // 2, P]
                some = slice(half * TILES // 2, (half + 1) * TILES // 2)
                nc.vector.tensor_tensor(to[half], col[:].unsqueeze(1).broadcast_to(shape),
                                        slot_lo[:, m, some].unsqueeze(2).broadcast_to(shape),
                                        ALU.is_equal).then_inc(onehots_ready, 1)

            def split_ctx(e, half):
                dve.wait_ge(ctx_hi_ready, e + 1)
                lo, whole, hi = ctx_half(e, half)
                nc.vector.tensor_tensor(lo, whole, hi.bitcast(F32), ALU.subtract).then_inc(ctx_lo_ready, 1)

            one_hot(in_lo_padded, 1, 0)
            one_hot(in_lo_padded, 1, 1)
            step(nc.vector.tensor_scalar(step_ge[:, 0, :], col[0:1, 0:STEPS], tot_before[0:1, 1, 1:2], None, ALU.is_ge))
            step(nc.vector.scalar_tensor_tensor(step_ge[:, 1, :], col[0:1, 0:STEPS], tot_before[0:1, 1, 2:3],
                                                step_ge[:, 0, :], ALU.is_ge, ALU.add))
            nc.vector.scalar_tensor_tensor(step_expert[:], col[0:1, 0:STEPS], tot_before[0:1, 1, 3:4],
                                           step_ge[:, 1, :], ALU.is_ge, ALU.add).then_inc(rows_ready, 1)
            dve.wait_ge(slots_ready, 1)
            nc.vector.tensor_copy(gather_row[:], p_sort[:, 0:STEPS]).then_inc(rows_ready, 1)
            step(nc.vector.tensor_scalar(empty[:], p_sort[:, 2 * STEPS:3 * STEPS], -1.0, 1.0, ALU.mult, ALU.add))
            step(nc.vector.tensor_tensor(empty_row[:], empty[:], pad_row[:], ALU.mult))
            nc.vector.tensor_tensor(x1_row[:], p_sort[:, STEPS:2 * STEPS], empty_row[:], ALU.add).then_inc(rows_ready, 1)
            split_ctx(0, 0)
            split_ctx(1, 0)

            def statistics(row, tile=None, between=None, first_use=False):
                r, half, parity = row
                if tile is None:
                    dve.wait_ge(x_landed[parity], 16 * (half + 1))
                else:
                    dve.wait_ge(x1_landed[tile[2]], 16 * (tile[1] + 1))
                nc.vector.bn_stats(bn6[:, parity, :], x_rows_of(r)).then_inc(bn6_ready, 1)
                dve.wait_ge(bn6_ready, r + 1)
                if between is not None:
                    normalise(between, first_use)
                nc.vector.bn_aggr(mean_var[:, parity, :], bn6[:, parity, :]).then_inc(mean_ready, 1)
                dve.wait_ge(mean_ready, r + 1)
                nc.vector.tensor_scalar(var_eps[:, parity:parity + 1], mean_var[:, parity, 1:2], EPS, None,
                                        ALU.add).then_inc(var_ready, 1)

            def normalise(row, first_use=False):
                r, _, parity = row
                dve.wait_ge(rstd_ready, r + 1)
                if not first_use:
                    dve.wait_ge(xT_ready, r - 1)
                nc.vector.tensor_scalar(xn[:, parity, :], x_rows_of(r), mean_var[:, parity, 0:1],
                                        rstd[:, parity:parity + 1], ALU.subtract, ALU.mult).then_inc(xn_ready, 1)

            def lo_x(r):
                dve.wait_ge(xhi_ready, r + 1)
                nc.vector.tensor_tensor(xT_lo[:], p_xT[:], xT_hi[:].bitcast(F32), ALU.subtract).then_inc(xlo_ready, 1)

            def lo_act(r, cols):
                dve.wait_ge(ahi_ready, r + 1)
                nc.vector.tensor_tensor(aT_lo[:, 0:cols], p_aT[:, 0:cols], aT_hi[:, 0:cols].bitcast(F32),
                                        ALU.subtract).then_inc(alo_ready, 1)

            def residual(row, first_use=False, y=p_y):
                r, half, parity = row
                dve.wait_ge(y_ready, r + 1)
                if not first_use:
                    dve.wait_ge(stored[parity], 16 * half)
                nc.vector.tensor_tensor(xout[:, parity, :], y[:], x_rows_of(r), ALU.add).then_inc(xout_ready, 1)

            def l1_gate(k, h=p_h):
                dve.wait_ge(silu_ready, k + 1)
                nc.vector.tensor_tensor(act[:, 0:D], silu[:], h[:], ALU.mult).then_inc(act_ready, 1)

            def l2_gates(t):
                of = 12 * t
                dve.wait_ge(part_a_ready, t + 1)
                nc.vector.tensor_copy(logits[:], p_a[:, ROUTE0:ROUTE0 + E2]).then_inc(router_step, 1)
                dve.wait_ge(router_step, of + 1)
                nc.vector.tensor_reduce(top1[:], logits[:], AX_X, ALU.max).then_inc(router_step, 1)
                nc.vector.max(top8[:], logits[:]).then_inc(router_step, 1)
                dve.wait_ge(router_step, of + 3)
                nc.vector.tensor_scalar(z[:], logits[:], top1[:, 0:1], -1.0, ALU.subtract, ALU.add).then_inc(z_ready, 1)
                nc.vector.max_index(top8_at[:], top8[:], logits[:]).then_inc(router_step, 1)
                dve.wait_ge(router_step, of + 4)
                nc.vector.tensor_scalar(chosen1[:], col[:, 0:E2], top8_at[:, 0:1], None,
                                        ALU.is_equal).then_inc(router_step, 1)
                dve.wait_ge(router_step, of + 5)
                nc.vector.scalar_tensor_tensor(chosen[:], col[:, 0:E2], top8_at[:, 1:2], chosen1[:],
                                               ALU.is_equal, ALU.add).then_inc(router_step, 1)
                dve.wait_ge(z_silu_ready, t + 1)
                nc.vector.tensor_tensor(z_rest[:], z[:], z_silu[:], ALU.subtract).then_inc(router_step, 1)
                dve.wait_ge(router_step, of + 7)
                nc.vector.reciprocal(z_rest_inv[:], z_rest[:]).then_inc(router_step, 1)
                dve.wait_ge(router_step, of + 8)
                nc.vector.tensor_tensor(z_exp[:], z_silu[:], z_rest_inv[:], ALU.mult).then_inc(router_step, 1)
                dve.wait_ge(router_step, of + 9)
                nc.vector.tensor_reduce(z_sum[:], z_exp[:], AX_X, ALU.add).then_inc(router_step, 1)
                dve.wait_ge(router_step, of + 10)
                nc.vector.reciprocal(z_sum_inv[:], z_sum[:]).then_inc(router_step, 1)
                dve.wait_ge(router_step, of + 11)
                nc.vector.scalar_tensor_tensor(gates[:], z_exp[:], z_sum_inv[:, 0:1], chosen[:],
                                               ALU.mult, ALU.mult).then_inc(router_step, 1)
                dve.wait_ge(router_step, of + 12)

            def l2_act(r, t):
                by_expert = "p (e f) -> p e f"
                half = E2 // 2
                nc.vector.tensor_tensor(act[:, HID:DN].rearrange(by_expert, e=E2),
                                        p_a[:, 0:LORA].rearrange(by_expert, e=E2),
                                        gates[:].unsqueeze(2).broadcast_to([P, E2, LR]), ALU.mult)
                nc.vector.tensor_tensor(up_gated[:, 0:HID // 2].rearrange(by_expert, e=half),
                                        p_a[:, UP_A0:GATE_B0].rearrange(by_expert, e=half),
                                        gates[:, 0:half].unsqueeze(2).broadcast_to([P, half, FE]), ALU.mult)
                dve.wait_ge(silu_b_ready, t + 1)
                nc.vector.tensor_tensor(up_gated[:, HID // 2:HID].rearrange(by_expert, e=half),
                                        p_b[:, UP_B0 - GATE_B0:GATE_C0 - GATE_B0].rearrange(by_expert, e=half),
                                        gates[:, half:E2].unsqueeze(2).broadcast_to([P, half, FE]),
                                        ALU.mult).then_inc(up_gated_ready, 1)
                dve.wait_ge(up_gated_ready, t + 1)
                dve.wait_ge(silu_ready, r + 1)
                nc.vector.tensor_tensor(act[:, 0:HID], silu[:], up_gated[:], ALU.mult).then_inc(act_ready, 1)

            statistics(one(0))
            statistics(one(1), between=one(0), first_use=True)
            split_ctx(1, 1)
            lo_x(0)
            normalise(one(1), first_use=True)
            split_ctx(2, 0)
            statistics(one(2))
            split_ctx(2, 1)
            dve.wait_ge(h_ready, 1)
            lo_x(1)
            l1_gate(0, p_a)
            statistics(one(3), between=one(2))
            lo_act(0, D)
            l1_gate(1)
            lo_x(2)
            one_hot(in_lo_compact, 0, 0)
            statistics(one(4), between=one(3))
            for k in range(2, 4):
                lo_act(k - 1, D)
                residual(one(k - 2), first_use=True)
                statistics(one(k + 3), between=one(k + 2))
                l1_gate(k)
                lo_x(k + 1)
                if k == 2:
                    step(nc.vector.tensor_tensor(in_tile[:], col[:, 0:TILES].unsqueeze(1).broadcast_to(to_tiles),
                                                 slot_hi[:, 0].unsqueeze(2).broadcast_to(to_tiles), ALU.is_equal))
                    nc.vector.tensor_tensor(put_compact[:], in_tile[:],
                                            token_f[:].unsqueeze(2).broadcast_to(to_tiles), ALU.mult)
                else:
                    dve.wait_ge(ctx_lo_ready, 2 * E1 - 1)
                    one_hot(in_lo_compact, 0, 1)
            with dve.Fori(2, (STEPS - 3) // 2) as h:
                for u in range(2):
                    k = 2 * h + u
                    lo_act(k - 1, D)
                    residual(pair(h, u - 2))
                    statistics(pair(h, u + 3), between=pair(h, u + 2))
                    l1_gate(k)
                    lo_x(k + 1)
            for k in range(STEPS - 3, STEPS):
                lo_act(k - 1, D)
                residual(one(k - 2))
                if k == STEPS - 3:
                    dve.wait_ge(slots_ready, 2)
                    nc.vector.tensor_copy(out_row[:], p_sort[:, COMPACT0:COMPACT0 + TILES]).then_inc(rows_ready, 1)
                statistics(one(k + 3), tile=one(k + 3 - STEPS), between=one(k + 2))
                l1_gate(k)
                lo_x(k + 1)

            r = STEPS
            lo_act(r - 1, D)
            residual(one(r - 2))
            statistics(one(r + 3), tile=one(3), between=one(r + 2))
            l2_gates(0)
            l2_act(r, 0)
            lo_x(r + 1)
            with dve.Fori(0, (TILES - 4) // 2) as h:
                for u in range(2):
                    t = 2 * h + u + 1
                    c = STEPS + 1 + u
                    lo_act(2 * h + c - 1, DN)
                    residual(pair(h, c - 2))
                    statistics(pair(h, c + 3), tile=pair(h, u + 4), between=pair(h, c + 2))
                    l2_gates(t)
                    l2_act(2 * h + c, t)
                    lo_x(2 * h + c + 1)
            for t in range(TILES - 3, TILES):
                r = STEPS + t
                lo_act(r - 1, DN)
                residual(one(r - 2))
                if r + 2 < ROWS:
                    normalise(one(r + 2))
                l2_gates(t)
                l2_act(r, t)
                if r + 1 < ROWS:
                    lo_x(r + 1)
            dve.wait_ge(y_ready, ROWS - 1)
            lo_act(ROWS - 1, DN)
            residual(one(ROWS - 2))
            residual(one(ROWS - 1), y=p_h)

        @block.tensor
        def _(pe):
            pe.wait_ge(masks_ready, 2)
            pe.wait_ge(counts_ready, 1)
            nc.tensor.matmul(p_sort[:, 0:E1], below[:], counts[:], start=True, stop=True)
            nc.tensor.matmul(p_sort[:, E1:2 * E1], ones[:], counts[:], start=True, stop=True).then_inc(offsets_ready, 1)
            def slots(to, in_lo, put, onehots_before):
                for c in range(TILES):
                    half, place = divmod(c, TILES // 2)
                    if place == 0:
                        pe.wait_ge(onehots_ready, onehots_before + half + 1)
                    last = nc.tensor.matmul(to, in_lo[half][:, place, :], put[:, c], start=(c == 0), stop=(c == TILES - 1))
                last.then_inc(slots_ready, 1)

            pe.wait_ge(puts_ready, 2)
            slots(p_sort[:, 0:3 * STEPS], in_lo_padded, put_padded[:].rearrange("p c v s -> p c (v s)"), 0)
            for _ in range(WARM):
                nc.tensor.matmul(p_y[:, 0:P], ones[:], below[:], start=True, stop=True)

            def blk(i):
                return slice(i * P, (i + 1) * P)

            def turn_x(r, parity):
                pe.wait_ge(xn_ready, r + 1)
                for i in range(KB):
                    last = nc.tensor.transpose(p_xT[:, blk(i)], xn[:, parity, blk(i)], ident[:])
                last.then_inc(xT_ready, 1)

            def turn_act(r, blocks):
                pe.wait_ge(act_ready, r + 1)
                for i in range(blocks):
                    last = nc.tensor.transpose(p_aT[:, blk(i)], act[:, blk(i)], ident[:])
                last.then_inc(aT_ready, 1)

            def hi_passes(to, hi, blocks, w_hi, w_lo):
                for i in range(blocks):
                    nc.tensor.matmul(to, hi[:, blk(i)], w_hi(i), start=(i == 0), stop=False)
                    nc.tensor.matmul(to, hi[:, blk(i)], w_lo(i), start=False, stop=False)

            def lo_passes(to, lo, blocks, w_hi):
                for i in range(blocks):
                    last = nc.tensor.matmul(to, lo[:, blk(i)], w_hi(i), start=False, stop=(i == blocks - 1))
                return last

            def l1_matrix(k):
                e = pe.value_load(step_expert[0:1, bass.ds(k, 1)], min_val=0, max_val=E1 - 1)
                return e, [lambda i, w=w: w[:, bass.ds(e * KB + i, 1), :].rearrange("p a f -> p (a f)")
                           for w in (ctx_hi, ctx_lo)]

            def l1_first(k, to=p_h, between=None, some_split=False):
                e, w = l1_matrix(k)
                if some_split:
                    pe.wait_ge(ctx_lo_ready, 2 * e + 1)
                pe.wait_ge(xhi_ready, k + 1)
                hi_passes(to[:], xT_hi, KB, *w)
                if between is not None:
                    between()
                pe.wait_ge(xlo_ready, k + 1)
                lo_passes(to[:], xT_lo, KB, w[0]).then_inc(h_ready, 1)

            def l1_second(k, first_use=False):
                e, w = l1_matrix(k)
                if not first_use:
                    pe.wait_ge(xout_ready, k)
                pe.wait_ge(ahi_ready, k + 1)
                hi_passes(p_y[:], aT_hi, KB, *w)
                pe.wait_ge(alo_ready, k + 1)
                lo_passes(p_y[:], aT_lo, KB, w[0]).then_inc(y_ready, 1)

            def up_part(c0, c1):
                return [lambda i, w=w: w[:, i * UPW + c0:i * UPW + c1] for w in (w2_hi, w2_lo)]

            down = [lambda i, w=w: w[:, DOWN0 + i * D:DOWN0 + (i + 1) * D] for w in (w2_hi, w2_lo)]

            def l2_first(r):
                pe.wait_ge(xhi_ready, r + 1)
                for to, c0, c1, ready in ((p_a, 0, GATE_B0, part_a_ready), (p_b, GATE_B0, GATE_C0, part_b_ready),
                                          (p_h, GATE_C0, UPW, part_c_ready)):
                    w = up_part(c0, c1)
                    hi_passes(to[:, 0:c1 - c0], xT_hi, KB, *w)
                    pe.wait_ge(xlo_ready, r + 1)
                    lo_passes(to[:, 0:c1 - c0], xT_lo, KB, w[0]).then_inc(ready, 1)

            def l2_second(r, to=p_y, between=None):
                if to is p_y:
                    pe.wait_ge(xout_ready, r)
                pe.wait_ge(ahi_ready, r + 1)
                hi_passes(to[:], aT_hi, DB, *down)
                pe.wait_ge(alo_ready, r + 1)
                if between is not None:
                    between()
                lo_passes(to[:], aT_lo, DB, down[0]).then_inc(y_ready, 1)

            pe.wait_ge(rows_ready, 1)

            def turn_x1():
                pe.wait_ge(xlo_ready, 1)
                turn_x(1, 1)

            turn_x(0, 0)
            pe.wait_ge(ctx_lo_half_ready, 1)
            l1_first(0, to=p_a, between=turn_x1, some_split=True)
            l1_first(1, between=lambda: turn_act(0, KB), some_split=True)
            turn_x(2, 0)
            l1_second(0, first_use=True)
            for k in range(2, 5):
                turn_act(k - 1, KB)
                l1_first(k, some_split=True)
                turn_x(k + 1, (k + 1) % 2)
                l1_second(k - 1)
            slots(p_sort[:, COMPACT0:COMPACT0 + TILES], in_lo_compact, put_compact, 2)
            pe.wait_ge(ctx_lo_ready, 2 * E1 - 1)
            with pe.Fori(2, (STEPS - 1) // 2) as h:
                for u in range(1, 3):
                    k = 2 * h + u
                    turn_act(k - 1, KB)
                    l1_first(k)
                    turn_x(k + 1, (u + 1) % 2)
                    l1_second(k - 1)
            turn_act(STEPS - 1, KB)
            pe.wait_ge(w2_lo_ready, -(-DOWN0 // PIECE))
            l2_first(STEPS)
            turn_x(STEPS + 1, (STEPS + 1) % 2)
            pe.wait_ge(w2_lo_ready, PIECES)
            l1_second(STEPS - 1)
            with pe.Fori(0, (TILES - 2) // 2) as h:
                for u in range(2):
                    r = 2 * h + STEPS + 1 + u
                    turn_act(r - 1, DB)
                    l2_first(r)
                    turn_x(r + 1, (STEPS + 2 + u) % 2)
                    l2_second(r - 1)
            turn_act(ROWS - 2, DB)
            l2_first(ROWS - 1)
            l2_second(ROWS - 2, between=lambda: turn_act(ROWS - 1, DB))
            l2_second(ROWS - 1, to=p_h)


def kernel(x, itok_BxS_13_99985, ctx_2048, L0_ffn_G, L0_ffn_gate_w, L0_ffn_up_w, L0_ffn_down_w, L0_ffn_lora_A,
           L0_ffn_lora_B):
    import numpy as np
    import concourse.bacc as bacc
    from concourse.bass_utils import run_bass_kernel_spmd

    def blocks(m):
        return np.ascontiguousarray(m.reshape(-1, P, m.shape[-1]).transpose(1, 0, 2)).reshape(P, -1)

    ctx = np.asarray(ctx_2048)
    gate, up, lora_a = (np.asarray(a).reshape(-1, D).T for a in (L0_ffn_gate_w, L0_ffn_up_w, L0_ffn_lora_A))
    down, lora_b = (np.asarray(a).transpose(0, 2, 1).reshape(-1, D) for a in (L0_ffn_down_w, L0_ffn_lora_B))
    arrays = {
        "x": np.ascontiguousarray(np.asarray(x).reshape(TOKENS, D)),
        "token_ids": np.ascontiguousarray(np.asarray(itok_BxS_13_99985).reshape(P, TILES)),
        "ctx_t": np.ascontiguousarray(
            ctx.transpose(0, 2, 1).reshape(E1, KB, P, D).transpose(2, 0, 1, 3)).reshape(P, E1, CTX),
        "w_up": blocks(np.concatenate([lora_a, np.asarray(L0_ffn_G), up[:, :HID // 2], gate[:, GATED_B:],
                                       up[:, HID // 2:], gate[:, :GATED_B]], axis=1)),
        "w_down": blocks(np.concatenate([down, lora_b], axis=0)),
    }
    nc = bacc.Bacc("TRN2", target_bir_lowering=False, num_devices=1)
    args = [nc.dram_tensor(n, a.shape, mybir.dt.from_np(a.dtype), kind="ExternalInput").ap() for n, a in arrays.items()]
    out = nc.dram_tensor("out", [TOKENS, D], F32, kind="ExternalOutput").ap()
    build(nc, *args, out)
    result = run_bass_kernel_spmd(nc, [arrays], core_ids=[0])
    return result.results[0]["out"].reshape(4, 512, D)
```
